# Optimizing a Trainium2 kernel written in Bass

```python
import numpy as np
import jax
import jax.numpy as jnp

def _softmax(x, axis=-1):
    return jax.nn.softmax(x, axis=axis)

def _gelu(x):
    return jax.nn.gelu(x, approximate=True)

def _silu(x):
    return jax.nn.silu(x)

def _sigmoid(x):
    return jax.nn.sigmoid(x)

def _layernorm(x, axis=-1, eps=1e-05):
    m = jnp.mean(x, axis=axis, keepdims=True)
    v = jnp.var(x, axis=axis, keepdims=True)
    return (x - m) / jnp.sqrt(v + eps)

def _scatter_add(tgt, idx, src, axis=0):
    return tgt.at[idx].add(src)

def _segment_sum(src, seg, n):
    return jax.ops.segment_sum(src, seg, n)
kernel_name = 'mk_flamingo_gated_d1_seqx_r4_92a3e9'

def setup_inputs(seed: int=0):
    np.random.seed(seed)
    _w = jnp.asarray

    def _rec_inputs():
        import jax
        import jax.numpy as jnp
        _rk = jax.random.key(seed)
        x = 7.22e-05 + 1 * jax.random.normal(jax.random.fold_in(_rk, 1), (16, 128, 1024), jnp.float32)
        _lenS = 128 - jax.random.randint(jax.random.fold_in(_rk, 7), (16,), 0, max(1, 128 // 4) + 1, jnp.int32)
        _lenS2 = 128 - jax.random.randint(jax.random.fold_in(_rk, 8), (16,), 0, max(1, 128 // 4) + 1, jnp.int32)
        _ctx_4096P = jax.random.normal(jax.random.fold_in(_rk, 11), (16, 16, 1024), jnp.float32)
        _ctx_4096c = jax.random.dirichlet(jax.random.fold_in(_rk, 511), 0.3 * jnp.ones((16,), jnp.float32), (16, 128))
        _ctx_4096t = jnp.einsum('bsk,bkd->bsd', _ctx_4096c, _ctx_4096P)
        _ctx_4096t = _ctx_4096t * jax.lax.rsqrt(jnp.mean(jnp.square(_ctx_4096t)) + 1e-12) * 0.953939
        ctx_4096 = 4.13588e-05 + 0.999923 * (_ctx_4096t + 0.3 * jax.random.normal(jax.random.fold_in(_rk, 611), (16, 128, 1024), jnp.float32))
        _g = jax.random.normal(jax.random.fold_in(_rk, 9001), (2, 1), jnp.float32)
        _g = jnp.sign(_g) * jnp.maximum(jnp.abs(_g), 1.0) + (_g == 0) * 1.0
        g_xattn = _g[0]
        g_ffn = _g[1]
        return (x, ctx_4096, g_xattn, g_ffn)
    x, ctx_4096, g_xattn, g_ffn = _rec_inputs()

    def _L0_xattn_setup():
        import jax, jax.numpy as jnp
        import numpy as np
        HEADS = 8
        WINDOW = 16

        def _pointwise(W, b, t):
            return jnp.einsum('oc,bct->bot', W, t) + b[None, :, None]
        key = jax.random.key(seed)
        ks = jax.random.split(key, 10)
        B, C, T = (4, 128, 1024)
        s = 0.02
        return {'x': jax.random.normal(ks[0], (B, C, T), jnp.float32), 'cond': jax.random.normal(ks[1], (B, C, T), jnp.float32), 'Wq': jax.random.normal(ks[2], (C, C), jnp.float32) * s, 'bq': jnp.zeros((C,), jnp.float32), 'Wk': jax.random.normal(ks[3], (C, C), jnp.float32) * s, 'bk': jnp.zeros((C,), jnp.float32), 'Wv': jax.random.normal(ks[4], (C, C), jnp.float32) * s, 'bv': jnp.zeros((C,), jnp.float32), 'Wo': jax.random.normal(ks[5], (C, C), jnp.float32) * s, 'bo': jnp.zeros((C,), jnp.float32)}
    _L0_xattn_all = _L0_xattn_setup()
    _L0_xattn_in = {k: v for k, v in _L0_xattn_all.items() if k in ('Wq', 'bq', 'Wk', 'bk', 'Wv', 'bv', 'Wo', 'bo')}
    del _L0_xattn_all

    def _L0_ffn_setup():
        import jax, jax.numpy as jnp
        import numpy as np
        GROUP_SIZE = 128

        def dequantize(imatrix, scales, zeros, group_size, out_dtype):
            rs = jnp.repeat(scales, group_size, axis=0)
            rz = jnp.repeat(zeros, group_size, axis=0)
            return ((imatrix.astype(rs.dtype) - rz.astype(rs.dtype)) * rs).astype(out_dtype)
        key = jax.random.key(seed)
        ks = jax.random.split(key, 10)
        H, I, G = (1024, 3584, GROUP_SIZE)
        B, S = (4, 512)
        x = jax.random.normal(ks[0], (B, S, H), dtype=jnp.float32)
        gate_w = jax.random.randint(ks[1], (H, I), 0, 16, dtype=jnp.int32)
        gate_z = jax.random.randint(ks[2], (H // G, I), 0, 16, dtype=jnp.int32)
        gate_s = jax.random.uniform(ks[3], (H // G, I), dtype=jnp.float32) * 0.01
        up_w = jax.random.randint(ks[4], (H, I), 0, 16, dtype=jnp.int32)
        up_z = jax.random.randint(ks[5], (H // G, I), 0, 16, dtype=jnp.int32)
        up_s = jax.random.uniform(ks[6], (H // G, I), dtype=jnp.float32) * 0.01
        down_w = jax.random.randint(ks[7], (I, H), 0, 16, dtype=jnp.int32)
        down_z = jax.random.randint(ks[8], (I // G, H), 0, 16, dtype=jnp.int32)
        down_s = jax.random.uniform(ks[9], (I // G, H), dtype=jnp.float32) * 0.01
        return {'x': x, 'gate_w': gate_w, 'gate_z': gate_z, 'gate_s': gate_s, 'up_w': up_w, 'up_z': up_z, 'up_s': up_s, 'down_w': down_w, 'down_z': down_z, 'down_s': down_s}
    _L0_ffn_all = _L0_ffn_setup()
    _L0_ffn_in = {k: v for k, v in _L0_ffn_all.items() if k in ('gate_w', 'gate_z', 'gate_s', 'up_w', 'up_z', 'up_s', 'down_w', 'down_z', 'down_s')}
    del _L0_ffn_all
    return {'x': x, 'ctx_4096': ctx_4096, 'g_xattn': g_xattn, 'g_ffn': g_ffn, 'L0_xattn_Wq': _L0_xattn_in['Wq'], 'L0_xattn_bq': _L0_xattn_in['bq'], 'L0_xattn_Wk': _L0_xattn_in['Wk'], 'L0_xattn_bk': _L0_xattn_in['bk'], 'L0_xattn_Wv': _L0_xattn_in['Wv'], 'L0_xattn_bv': _L0_xattn_in['bv'], 'L0_xattn_Wo': _L0_xattn_in['Wo'], 'L0_xattn_bo': _L0_xattn_in['bo'], 'L0_ffn_gate_w': _L0_ffn_in['gate_w'], 'L0_ffn_gate_z': _L0_ffn_in['gate_z'], 'L0_ffn_gate_s': _L0_ffn_in['gate_s'], 'L0_ffn_up_w': _L0_ffn_in['up_w'], 'L0_ffn_up_z': _L0_ffn_in['up_z'], 'L0_ffn_up_s': _L0_ffn_in['up_s'], 'L0_ffn_down_w': _L0_ffn_in['down_w'], 'L0_ffn_down_z': _L0_ffn_in['down_z'], 'L0_ffn_down_s': _L0_ffn_in['down_s']}

def reference(x, ctx_4096, g_xattn, g_ffn, L0_xattn_Wq, L0_xattn_bq, L0_xattn_Wk, L0_xattn_bk, L0_xattn_Wv, L0_xattn_bv, L0_xattn_Wo, L0_xattn_bo, L0_ffn_gate_w, L0_ffn_gate_z, L0_ffn_gate_s, L0_ffn_up_w, L0_ffn_up_z, L0_ffn_up_s, L0_ffn_down_w, L0_ffn_down_z, L0_ffn_down_s):
    import jax
    import jax.numpy as jnp

    def _L0_xattn_ref(x, cond, Wq, bq, Wk, bk, Wv, bv, Wo, bo):
        import jax, jax.numpy as jnp
        import numpy as np
        HEADS = 8
        WINDOW = 16

        def _pointwise(W, b, t):
            return jnp.einsum('oc,bct->bot', W, t) + b[None, :, None]
        B, C, T = x.shape
        H, W = (HEADS, WINDOW)
        hd = C // H
        scale = hd ** (-0.5)
        pad_left = W // 2
        pad_right = W - pad_left - 1
        q = _pointwise(Wq, bq, x)
        k = _pointwise(Wk, bk, cond)
        v = _pointwise(Wv, bv, cond)
        k = jnp.pad(k, ((0, 0), (0, 0), (pad_left, pad_right)))
        v = jnp.pad(v, ((0, 0), (0, 0), (pad_left, pad_right)))
        idx = jnp.arange(T)[:, None] + jnp.arange(W)[None, :]
        k_win = k[:, :, idx].reshape(B, H, hd, T, W)
        v_win = v[:, :, idx].reshape(B, H, hd, T, W)
        qh = q.reshape(B, H, hd, T)
        dots = jnp.einsum('bhdt,bhdtw->bhtw', qh, k_win) * scale
        attn = jax.nn.softmax(dots, axis=-1)
        out = jnp.einsum('bhtw,bhdtw->bhdt', attn, v_win)
        out = out.reshape(B, C, T)
        return _pointwise(Wo, bo, out)

    def _L0_ffn_ref(x, gate_w, gate_z, gate_s, up_w, up_z, up_s, down_w, down_z, down_s):
        import jax, jax.numpy as jnp
        import numpy as np
        GROUP_SIZE = 128

        def dequantize(imatrix, scales, zeros, group_size, out_dtype):
            rs = jnp.repeat(scales, group_size, axis=0)
            rz = jnp.repeat(zeros, group_size, axis=0)
            return ((imatrix.astype(rs.dtype) - rz.astype(rs.dtype)) * rs).astype(out_dtype)
        dt = x.dtype
        gate_proj = dequantize(gate_w, gate_s, gate_z, GROUP_SIZE, dt)
        up_proj = dequantize(up_w, up_s, up_z, GROUP_SIZE, dt)
        down_proj = dequantize(down_w, down_s, down_z, GROUP_SIZE, dt)
        gate = jax.nn.silu(jnp.dot(x, gate_proj))
        up = jnp.dot(x, up_proj)
        return jnp.dot(gate * up, down_proj)
    x = x + jnp.tanh(g_xattn[0]) * _L0_xattn_ref(_layernorm(x, axis=-1), ctx_4096, L0_xattn_Wq, L0_xattn_bq, L0_xattn_Wk, L0_xattn_bk, L0_xattn_Wv, L0_xattn_bv, L0_xattn_Wo, L0_xattn_bo)
    x = x + jnp.tanh(g_ffn[0]) * _L0_ffn_ref(_layernorm(x, axis=-1), L0_ffn_gate_w, L0_ffn_gate_z, L0_ffn_gate_s, L0_ffn_up_w, L0_ffn_up_z, L0_ffn_up_s, L0_ffn_down_w, L0_ffn_down_z, L0_ffn_down_s)
    return x

_drawn_inputs = setup_inputs


def setup_inputs(seed=0):
    import zlib

    import numpy as np

    out = dict(_drawn_inputs(seed))
    spreads = {'L0_xattn_bq': (0.0, 2.0),
     'L0_xattn_bk': (0.0, 2.0),
     'L0_xattn_bv': (0.0, 0.8),
     'L0_xattn_bo': (0.0, 0.1)}
    factors = {'L0_xattn_Wq': 8.0, 'L0_xattn_Wk': 8.0}
    for name, (base, spread) in spreads.items():
        noise = np.random.default_rng([zlib.crc32(name.encode()), seed]).standard_normal(out[name].shape)
        drawn = base * np.exp(spread * noise) if base else spread * noise
        out[name] = jnp.asarray(drawn.astype(out[name].dtype))
    for name, factor in factors.items():
        out[name] = (out[name] * factor).astype(out[name].dtype)
    return out
```

```python
import concourse.bass as bass
from concourse import mybir
from contextlib import ExitStack


def flamingo_layer(nc, x_in, ctx_in, g_xattn, g_ffn, WqT, bq, WkT, bk, WvT, bv, WoT, bo,
                   gate_w, gate_z, gate_s, up_w, up_z, up_s, down_w, down_z, down_s, out):
    fp32, fp16, bf16, i32 = mybir.dt.float32, mybir.dt.float16, mybir.dt.bfloat16, mybir.dt.int32
    ALU, ACT, AX = mybir.AluOpType, mybir.ActivationFunctionType, mybir.AxisListType
    P = 128

    B, C, T = x_in.shape
    HEADS, WIN = 8, 16
    HD = C // HEADS
    PAD = WIN // 2
    QB = 32
    KW = QB + WIN
    KP = 64
    NJ = T // QB
    HG = 4
    GC = HG * HD
    NQ = 4
    JQ = NJ // NQ
    PQ = JQ // 2
    G = NQ * 2
    HALF = 512
    EPS = 1e-5
    MASKED = -1e30

    F = gate_w.shape[1]
    NK = T // P
    SC = 2
    NC = F // (P * SC)
    ROWS = B * C
    TB = 512
    NT = ROWS // TB
    TT = TB // P
    XS = 256.0
    WS = 4096.0
    NPC = 3 * SC

    ctx = ExitStack()
    with ctx:
        def sb(name, shape, dt, stack=ctx):
            return stack.enter_context(nc.sbuf_tensor(name, shape, dt))

        def sem(name):
            return ctx.enter_context(nc.semaphore(name))

        rows = sb("rows", [P, B, T], fp32)
        xT_hi = sb("xT_hi", [P, NK, ROWS], fp16)
        xT_lo = sb("xT_lo", [P, NK, ROWS], fp16)
        gates = sb("gates", [P, 2], fp32)
        tanh_g = sb("tanh_g", [P, 2], fp32)
        ffn_gate = sb("ffn_gate", [P, 1], fp32)

        att = ExitStack()
        wq = sb("wq", [P, C], fp32, att)
        wk = sb("wk", [P, C], fp32, att)
        wv = sb("wv", [P, C], fp32, att)
        wo = sb("wo", [P, 2, 2, C], fp32, att)
        bias = sb("bias", [P, 3], fp32, att)
        bq4 = sb("bq4", [P, 1], fp32, att)
        bo_g = sb("bo_g", [P, 1], fp32, att)
        bv_all = sb("bv_all", [P, C], fp32, att)
        CW = PAD + T + 24
        head_of = sb("head_of", [P, HG], fp32, att)
        ident = sb("ident", [P, P], fp32, att)
        spread = sb("spread", [P, HG, QB], bf16, att)
        window = sb("window", [P, KW], bf16, att)
        xt = sb("xt", [P, T], fp32, att)
        ct = sb("ct", [P, CW], fp32, att)
        xn = sb("xn", [P, T], fp32, att)
        stats = sb("stats", [P, 2, 2, 6], fp32, att)
        mv = sb("mv", [P, 2, 2], fp32, att)
        var_eps = sb("var_eps", [P, 2], fp32, att)
        minus_half = sb("minus_half", [P, 1], fp32, att)
        rstd = sb("rstd", [P, 2], fp32, att)
        qt = sb("qt", [P, T], fp32, att)
        qm = sb("qm", [P, NJ, HG, QB], fp32, att)
        kt = sb("kt", [P, 2, T + WIN], fp32, att)
        vt = sb("vt", [P, 2, NJ // 2, C], fp32, att)
        pr = sb("pr", [P, 2, JQ, KP], fp32, att)
        pT = sb("pT", [P, 2, HALF], fp32, att)
        rmax = sb("rmax", [P, 2, JQ], fp32, att)
        rsum = sb("rsum", [P, 2, NJ], fp32, att)
        rinv = sb("rinv", [P, 2 * NJ], fp32, att)
        on = sb("on", [P, 2, NJ // 2, 2, HD], fp32, att)
        shared = sb("shared", [P, 9 * C], fp32, att)
        oT = shared[:, 0:T].rearrange("p (g n) -> p g n", g=2)
        vn = shared[:, :].rearrange("p (n c) -> p n c", c=C)
        att.close()

        w_hi = sb("w_hi", [P, 2, SC, 2, NK, P], fp16)
        w_lo = sb("w_lo", [P, 2, SC, 2, NK, P], fp16)
        d_hi = sb("d_hi", [P, SC, T], fp16)
        d_lo = sb("d_lo", [P, SC, T], fp16)
        raw_w = sb("raw_w", [P, 2, NK, P], i32)
        raw_z = sb("raw_z", [P, 2, NK, P], i32)
        raw_s = sb("raw_s", [P, 2, NK, P], fp32)
        silu = sb("silu", [P, TB], fp32)
        hid = sb("hid", [P, TB], fp32)
        h_hi = sb("h_hi", [P, 2, SC, TB], fp16)
        h_lo = sb("h_lo", [P, 2, SC, TB], fp16)

        bank = [ctx.enter_context(nc.psum_tensor(f"bank{n}", [P, HALF], fp32)) for n in range(8)]
        proj = bank[0:2]
        score = bank[2:4]
        turned = bank[4:6]
        mixed = bank[6:8]
        gate_ps = bank[0:2]
        up_ps = bank[2:4]

        consts_loaded, gates_loaded = sem("consts_loaded"), sem("gates_loaded")
        zeroed, consts_made, masks_made, gates_ready, scaled_bias = (
            sem("zeroed"), sem("consts_made"), sem("masks_made"), sem("gates_ready"), sem("scaled_bias"))
        x_loaded, ctx_loaded, q_spread, v_placed = (
            sem("x_loaded"), sem("ctx_loaded"), sem("q_spread"), sem("v_placed"))
        residual_set = sem("residual_set")
        eps_added = [sem("eps_added"), sem("eps2_added")]
        stats_done, mv_done, rstd_done, x_normed = sem("stats_done"), sem("mv_done"), sem("rstd_done"), sem("x_normed")
        q_proj, k_proj, v_proj, o_proj, xT_ready = (
            sem("q_proj"), sem("k_proj"), sem("v_proj"), sem("o_proj"), sem("xT_ready"))
        q_ready, k_ready, v_ready = sem("q_ready"), sem("k_ready"), sem("v_ready")
        scores_ready, max_ready, shifted, probs_ready, sum_ready = (
            sem("scores_ready"), sem("max_ready"), sem("shifted"), sem("probs_ready"), sem("sum_ready"))
        probs_turned, pT_ready, pv_ready = sem("probs_turned"), sem("pT_ready"), sem("pv_ready")
        picked_act, picked_dve = sem("picked_act"), sem("picked_dve")
        rinv_ready, o_scaled, oT_ready, attended = (
            sem("rinv_ready"), sem("o_scaled"), sem("oT_ready"), sem("attended"))
        stats2_done, mv2_done, rstd2_done, row_normed = (
            sem("stats2_done"), sem("mv2_done"), sem("rstd2_done"), sem("row_normed"))
        hi_ready, lo_ready = sem("hi_ready"), sem("lo_ready")

        raw_loaded = [sem("raw0_loaded"), sem("raw1_loaded")]
        zero_taken, scaled, w_hi_ready, w_lo_ready = (
            sem("zero_taken"), sem("scaled"), sem("w_hi_ready"), sem("w_lo_ready"))
        gate_ready, up_ready, silu_ready, hid_ready, h_hi_ready, h_lo_ready = (
            sem("gate_ready"), sem("up_ready"), sem("silu_ready"), sem("hid_ready"), sem("h_hi_ready"),
            sem("h_lo_ready"))
        down_ready, added = sem("down_ready"), sem("added")
        stored = sem("stored")

        N_CONST = 7 + 16

        def batches(eng, batch):
            batch(0, 0, False, True)
            batch(1, 1, True, True)
            with eng.Fori(1, B // 2 - 1) as i:
                batch(2 * i, 0, True, True)
                batch(2 * i + 1, 1, True, True)
            batch(B - 2, 0, True, True)
            batch(B - 1, 1, True, False)

        def passes(eng, one):
            one(0, 0, True, False)
            with eng.Fori(0, (NC - 2) // 2) as i:
                one(2 * i + 1, 1, False, False)
                one(2 * i + 2, 0, False, False)
            one(NC - 1, 1, False, True)

        def first_wait(eng, *values):
            values = [v if isinstance(v, int) else eng.snap(eng.to_reg(v)) for v in values]
            eng.wait_ge(consts_made, 5)
            return values

        block = ctx.enter_context(nc.Block())

        @block.sync
        def _(sp):
            sp.dma_start(xt[:, :], x_in[0]).then_inc(x_loaded, 16)
            sp.dma_start(wq[:, :], WqT).then_inc(consts_loaded, 16)
            sp.dma_start(wk[:, :], WkT).then_inc(consts_loaded, 16)
            sp.dma_start(wv[:, :], WvT).then_inc(consts_loaded, 16)
            for n, v in enumerate((bq, bk, bo)):
                sp.dma_start(bias[:, n:n + 1], v.rearrange("(p a) -> p a", a=1)).then_inc(consts_loaded, 16)
            sp.dma_start(bv_all[:, :], bv.partition_broadcast(P)).then_inc(consts_loaded, 16)
            for n, v in enumerate((g_xattn, g_ffn)):
                sp.dma_start(gates[:, n:n + 1], v.partition_broadcast(P)).then_inc(gates_loaded, 16)
            sp.wait_ge(zeroed, 2)
            sp.dma_start(ct[:, PAD:PAD + T], ctx_in[0]).then_inc(ctx_loaded, 16)
            for h in range(HG):
                for hg in range(2):
                    for jj in range(2):
                        lo = QB * h + HD * jj
                        src = HD * (HG * hg + h)
                        sp.dma_start(wo[lo:lo + HD, hg, jj, :], WoT[src:src + HD, :])\
                          .then_inc(consts_loaded, 16)

            def place_v(b, par):
                ready, used = first_wait(sp, 3 * b + 3, G * (b - 1))
                sp.wait_ge(v_ready, ready)
                if not isinstance(b, int) or b > 1:
                    sp.wait_ge(pv_ready, used)
                E, O = slice(0, NJ // 2, 2), slice(1, NJ // 2, 2)
                for dst, src in (
                        (vt[PAD:KW, par, 0, :], vn[PAD:KW, 0, :]),
                        (vt[0:KW, par, 2:NJ // 2:2, :], vn[0:KW, 1:8, :]),
                        (vt[KP:KP + KW, par, E, :], vn[QB:QB + KW, 0:8, :]),
                        (vt[0:KW, par, O, :], vn[KP:KP + KW, 0:8, :]),
                        (vt[KP:KP + QB, par, O, :], vn[3 * QB:P, 0:8, :]),
                        (vt[KP + QB:KP + KW, par, 1:NJ // 2 - 1:2, :], vn[0:WIN, 1:8, :]),
                        (vt[KP + QB:KP + QB + PAD, par, NJ // 2 - 1, :], vn[0:PAD, 8, :])):
                    sp.dma_start(dst, src).then_inc(v_placed, 16)

            sp.wait_ge(zeroed, 3)
            place_v(0, 0)

            def batch(b, par, has_prev, has_next):
                if has_next:
                    used, = first_wait(sp, b + 1)
                    sp.wait_ge(x_normed, used)
                    sp.wait_ge(residual_set, used)
                    sp.dma_start(xt[:, :], x_in[bass.ds(b + 1, 1)].rearrange("a c t -> (a c) t"))\
                      .then_inc(x_loaded, 16)
                if has_next:
                    used, = first_wait(sp, 3 * b + 3)
                    sp.wait_ge(v_proj, used)
                    sp.dma_start(ct[:, PAD:PAD + T], ctx_in[bass.ds(b + 1, 1)].rearrange("a c t -> (a c) t"))\
                      .then_inc(ctx_loaded, 16)
                    place_v(b + 1, 1 - par)

            batches(sp, batch)

            def load_piece(c, n, first):
                slot = n % 2
                if first:
                    if slot == 0 and n == 0:
                        sp.wait_ge(attended, 2 * B)
                        sp.wait_ge(lo_ready, 2 * B)
                        sp.wait_ge(q_spread, 2 * B)
                        sp.wait_ge(xT_ready, 2 * B)
                        sp.wait_ge(v_placed, 112 * B)
                used, = first_wait(sp, NPC * c + n - 1)
                if not (first and n < 2):
                    sp.wait_ge(w_lo_ready, used)
                w, z, s = raw_w[:, slot], raw_z[:, slot], raw_s[:, slot]
                if n < 2 * SC:
                    ww, zz, ss = ((gate_w, gate_z, gate_s), (up_w, up_z, up_s))[n % 2]
                    col = (c * SC + n // 2) * P
                    src = ww[:, bass.ds(col, P)].rearrange("(k p) i -> p k i", p=P)
                    zrc = zz[:, bass.ds(col, P)].partition_broadcast(P)
                    src_s = ss[:, bass.ds(col, P)].partition_broadcast(P)
                else:
                    r = c * SC + n - 2 * SC
                    src = down_w[bass.ds(r * P, P), :].rearrange("p (k i) -> p k i", k=NK)
                    zrc = down_z[bass.ds(r, 1), :].rearrange("a (k i) -> (a k) i", k=NK).partition_broadcast(P)
                    src_s = down_s[bass.ds(r, 1), :].rearrange("a (k i) -> (a k) i", k=NK).partition_broadcast(P)
                sp.dma_start(w, src).then_inc(raw_loaded[slot], 16)
                sp.dma_start(z, zrc).then_inc(raw_loaded[slot], 16)
                sp.dma_start(s, src_s).then_inc(raw_loaded[slot], 16)

            for n in range(2 * SC):
                load_piece(0, n, True)

            def one(c, par, first, last):
                for n in range(2 * SC, NPC):
                    load_piece(c, n, False)
                if not last:
                    for n in range(2 * SC):
                        load_piece(c + 1, n, False)

            passes(sp, one)

            for t in range(B):
                sp.wait_ge(added, (NC - 1) * B + t + 1)
                sp.dma_start(out[t], rows[:, t, :]).then_inc(stored, 16)
            sp.wait_ge(stored, 16 * B)

        @block.gpsimd
        def _(pool):
            nc.gpsimd.memset(ct[:, :], 0.0).then_inc(zeroed, 1)
            nc.gpsimd.memset(wo[:, :, :, :], 0.0).then_inc(zeroed, 1)
            nc.gpsimd.memset(vt[:, :, :, :], 0.0).then_inc(zeroed, 1)
            nc.gpsimd.memset(kt[:, :, :], 0.0).then_inc(zeroed, 1)
            nc.gpsimd.memset(pr[:, :, :, :], 0.0).then_inc(zeroed, 1)
            nc.gpsimd.memset(head_of[:, :], 1.0).then_inc(consts_made, 1)
            nc.gpsimd.memset(minus_half[:, :], -0.5).then_inc(consts_made, 1)
            nc.gpsimd.memset(ident[:, :], 0.0).then_inc(consts_made, 1)
            nc.gpsimd.memset(spread[:, :, :], 0.0).then_inc(consts_made, 1)
            nc.gpsimd.memset(window[:, :], 0.0).then_inc(consts_made, 1)
            pool.wait_ge(consts_made, 5)
            nc.gpsimd.affine_select(out=ident[:, :], in_=ident[:, :], compare_op=ALU.not_equal, fill=1.0,
                                    base=0, pattern=[[-1, P]], channel_multiplier=1).then_inc(masks_made, 1)
            for n, lo in enumerate((0, GC)):
                sp_rows = spread[lo:lo + QB, :, :]
                nc.gpsimd.affine_select(out=sp_rows, in_=sp_rows, compare_op=ALU.not_equal, fill=1.0, base=0,
                                        pattern=[[0, HG], [-1, QB]], channel_multiplier=1).then_inc(masks_made, 1)
                win = window[lo:lo + QB, :]
                nc.gpsimd.affine_select(out=win, in_=win, compare_op=ALU.is_ge, fill=MASKED, base=0,
                                        pattern=[[1, KW]], channel_multiplier=-1).then_inc(masks_made, 1)
                pool.wait_ge(masks_made, 3 + 5 * n)
                nc.gpsimd.affine_select(out=win, in_=win, compare_op=ALU.is_ge, fill=MASKED, base=WIN - 1,
                                        pattern=[[-1, KW]], channel_multiplier=1).then_inc(masks_made, 1)
                mine = head_of[lo:lo + GC, :]
                nc.gpsimd.affine_select(out=mine, in_=mine, compare_op=ALU.is_ge, fill=0.0, base=0,
                                        pattern=[[-HD, HG]], channel_multiplier=1).then_inc(masks_made, 1)
                pool.wait_ge(masks_made, 5 + 5 * n)
                nc.gpsimd.affine_select(out=mine, in_=mine, compare_op=ALU.is_ge, fill=0.0, base=HD - 1,
                                        pattern=[[HD, HG]], channel_multiplier=-1).then_inc(masks_made, 1)
            pool.wait_ge(masks_made, 11)

            def spread_q(b, half):
                ready, used = first_wait(pool, 2 * b + half + 1, G * (b - 1) + (half + 1) * (G // 2))
                pool.wait_ge(q_ready, ready)
                if not isinstance(b, int) or b > 0:
                    pool.wait_ge(scores_ready, used)
                n = NJ // 2
                for h in range(HG):
                    last = nc.gpsimd.tensor_scalar(
                        qm[:, half * n:(half + 1) * n, h, :],
                        qt[:, half * HALF:(half + 1) * HALF].rearrange("p (j t) -> p j t", t=QB),
                        head_of[:, h:h + 1], None, ALU.mult)
                last.then_inc(q_spread, 1)

            def inverse_std(b, which, moments_ready, used, done):
                now, before = first_wait(pool, b + 1, b)
                pool.wait_ge(moments_ready, now)
                if not isinstance(b, int) or b > 0:
                    pool.wait_ge(used, before)
                nc.gpsimd.tensor_scalar(var_eps[:, which:which + 1], mv[:, which, 1:2], EPS, None, ALU.add)\
                    .then_inc(eps_added[which], 1)
                pool.wait_ge(eps_added[which], b + 1)
                nc.gpsimd.tensor_tensor(rstd[:, which:which + 1], var_eps[:, which:which + 1], minus_half[:, :],
                                        ALU.pow)\
                    .then_inc(done, 1)

            inverse_std(0, 0, mv_done, x_normed, rstd_done)
            spread_q(0, 0)

            def batch(b, par, has_prev, has_next):
                spread_q(b, 1)
                if has_next:
                    inverse_std(b + 1, 0, mv_done, x_normed, rstd_done)
                if has_prev:
                    inverse_std(b - 1, 1, mv2_done, row_normed, rstd2_done)
                if has_next:
                    spread_q(b + 1, 0)

            batches(pool, batch)
            inverse_std(B - 1, 1, mv2_done, row_normed, rstd2_done)

            def take_zero(c, n):
                slot = n % 2
                pool.wait_ge(raw_loaded[slot], (c * (NPC // 2) + n // 2 + 1) * 48)
                nc.gpsimd.tensor_tensor(raw_z[:, slot], raw_w[:, slot], raw_z[:, slot], ALU.subtract)\
                    .then_inc(zero_taken, 1)

            def low_weight(c, n, par):
                slot = n % 2
                pool.wait_ge(w_hi_ready, c * NPC + n + 1)
                if n < 2 * SC:
                    hi = w_hi[:, par, n // 2, n % 2].rearrange("p k i -> p (k i)")
                    lo = w_lo[:, par, n // 2, n % 2].rearrange("p k i -> p (k i)")
                else:
                    hi, lo = d_hi[:, n - 2 * SC, :], d_lo[:, n - 2 * SC, :]
                nc.gpsimd.tensor_tensor(lo, raw_s[:, slot].rearrange("p k i -> p (k i)"), hi, ALU.subtract)\
                    .then_inc(w_lo_ready, 1)

            take_zero(0, 0)
            for n in range(1, 2 * SC):
                take_zero(0, n)
                low_weight(0, n - 1, 0)

            def one(c, par, first, last):
                for n in range(2 * SC, NPC):
                    take_zero(c, n)
                    low_weight(c, n - 1, par)
                if last:
                    low_weight(c, NPC - 1, par)
                else:
                    take_zero(c + 1, 0)
                    low_weight(c, NPC - 1, par)
                    for n in range(1, 2 * SC):
                        take_zero(c + 1, n)
                        low_weight(c + 1, n - 1, 1 - par)

            passes(pool, one)

        @block.scalar
        def _(act):
            act.wait_ge(gates_loaded, 32)
            nc.scalar.activation(tanh_g[:, :], gates[:, :], ACT.Tanh).then_inc(gates_ready, 1)
            act.wait_ge(gates_ready, 1)
            nc.scalar.activation(ffn_gate[:, :], tanh_g[:, 1:2], ACT.Copy, scale=1.0 / WS).then_inc(scaled_bias, 1)
            act.wait_ge(consts_loaded, 16 * N_CONST)
            nc.scalar.activation(bq4[:, :], bias[:, 0:1], ACT.Copy, scale=HD ** -0.5).then_inc(scaled_bias, 1)
            nc.scalar.activation(bo_g[:, :], bias[:, 2:3], ACT.Identity, scale=tanh_g[:, 0:1]).then_inc(scaled_bias, 1)
            act.wait_ge(scaled_bias, 3)
            act.wait_ge(zeroed, 5)

            def set_residual(b):
                act.wait_ge(x_loaded, 16 * (b + 1))
                nc.scalar.activation(rows[:, bass.ds(b, 1), :].rearrange("p a t -> p (a t)"), xt[:, :], ACT.Identity,
                                     bias=bo_g[:, :]).then_inc(residual_set, 1)

            def take_q(b):
                for n in range(2):
                    act.wait_ge(q_proj, 2 * b + n + 1)
                    if not isinstance(b, int) or b > 0:
                        act.wait_ge(q_spread, 2 * b - 1 + n)
                    nc.scalar.activation(qt[:, n * HALF:(n + 1) * HALF], proj[n][:, :], ACT.Identity,
                                         bias=bq4[:, :], scale=HD ** -0.5).then_inc(q_ready, 1)

            def take_k(b, par):
                for n in range(2):
                    act.wait_ge(k_proj, 2 * b + n + 1)
                    nc.scalar.activation(kt[:, par, PAD + n * HALF:PAD + (n + 1) * HALF], proj[n][:, :],
                                         ACT.Identity, bias=bias[:, 1:2]).then_inc(k_ready, 1)

            def exp(b, g):
                act.wait_ge(shifted, G * b + g + 1)
                nc.scalar.activation(pr[:, g % 2, :, 0:KW], pr[:, g % 2, :, 0:KW], ACT.Exp)\
                    .then_inc(probs_ready, 1)

            def take_pT(b, g):
                act.wait_ge(probs_turned, G * b + g + 1)
                if not isinstance(b, int) or b > 0 or g >= 2:
                    act.wait_ge(pv_ready, G * b + g - 1)
                nc.scalar.activation(pT[:, g % 2, :], turned[g % 2][:, :], ACT.Copy).then_inc(pT_ready, 1)

            def pick(b, q):
                act.wait_ge(pv_ready, G * b + 2 * q + 2)
                if q == 0 and (not isinstance(b, int) or b > 0):
                    act.wait_ge(oT_ready, b)
                for h in range(2):
                    for jj in range(2):
                        src = mixed[jj].rearrange("p (g j c) -> p g j c", g=2, c=GC)
                        lo = QB * h
                        last = nc.scalar.activation(on[lo:lo + QB, :, q * PQ:(q + 1) * PQ, jj, :],
                                                    src[lo:lo + QB, :, :, HD * h:HD * h + HD], ACT.Copy)
                last.then_inc(picked_act, 1)

            def take_xT(b):
                for n in range(2):
                    act.wait_ge(xT_ready, 2 * b + n + 1)
                    dst = xT_hi[:, 4 * n:4 * n + 4, bass.ds(b * P, P)]
                    nc.scalar.activation(dst, proj[n].rearrange("p (k r) -> p k r", r=P), ACT.Copy, scale=XS)\
                        .then_inc(hi_ready, 1)

            set_residual(0)
            take_q(0)
            take_k(0, 0)

            def batch(b, par, has_prev, has_next):
                for g in range(G):
                    exp(b, g)
                    if g > 0:
                        take_pT(b, g - 1)
                    elif has_prev:
                        take_pT(b - 1, G - 1)
                    if g == 0 and has_next:
                        set_residual(b + 1)
                    if g == 1:
                        if has_prev:
                            pick(b - 1, 3)
                    if g == 2 and has_next:
                        take_q(b + 1)
                    if g >= 3 and g % 2 == 1:
                        pick(b, (g - 3) // 2)
                    if g == 4 and has_next:
                        take_k(b + 1, 1 - par)
                    if g == 7 and has_prev:
                        take_xT(b - 1)

            batches(act, batch)
            take_pT(B - 1, G - 1)
            pick(B - 1, 3)
            take_xT(B - 1)

            def cast_weight(c, n, par):
                act.wait_ge(scaled, c * NPC + n + 1)
                slot = n % 2
                if n < 2 * SC:
                    if not isinstance(c, int) or c >= 2:
                        act.wait_ge(up_ready, (c - 1) * NT * SC)
                    dst = w_hi[:, par, n // 2, n % 2].rearrange("p k i -> p (k i)")
                else:
                    if not isinstance(c, int) or c >= 1:
                        act.wait_ge(down_ready, c * B)
                    dst = d_hi[:, n - 2 * SC, :]
                nc.scalar.activation(dst, raw_s[:, slot].rearrange("p k i -> p (k i)"), ACT.Copy)\
                    .then_inc(w_hi_ready, 1)

            def hidden(c, t, i):
                u = (c * NT + t) * SC + i
                act.wait_ge(gate_ready, u + 1)
                if not isinstance(c, int) or c > 0 or t > 0 or i > 0:
                    act.wait_ge(hid_ready, u)
                nc.scalar.activation(silu[:, :], gate_ps[i][:, :], ACT.Silu, scale=1.0 / (XS * WS))\
                    .then_inc(silu_ready, 1)
                act.wait_ge(hid_ready, u + 1)
                if not isinstance(c, int) or c > 0 or t > 1:
                    act.wait_ge(down_ready, (c * NT + t - 1) * TT)
                nc.scalar.activation(h_hi[:, t % 2, i, :], hid[:, :], ACT.Copy).then_inc(h_hi_ready, 1)

            for n in range(2 * SC):
                cast_weight(0, n, 0)

            def one(c, par, first, last):
                for t in range(NT):
                    for i in range(SC):
                        hidden(c, t, i)
                        if t == 0:
                            pass
                    if t == 0:
                        for i in range(SC):
                            cast_weight(c, 2 * SC + i, par)
                    if t in (1, 2) and not last:
                        for n in range(2 * (t - 1), 2 * t):
                            cast_weight(c + 1, n, 1 - par)

            passes(act, one)

        @block.vector
        def _(dve):
            dve.wait_ge(gates_ready, 1)

            def moments(b, src, which, s_stats, s_mv):
                for n in range(2):
                    nc.vector.bn_stats(out=stats[:, which, n, :], in_=src(n)).then_inc(s_stats, 1)
                both, = first_wait(dve, 2 * b + 2)
                dve.wait_ge(s_stats, both)
                nc.vector.bn_aggr(out=mv[:, which, :], in_=stats[:, which, :, :]).then_inc(s_mv, 1)

            def moments_x(b):
                loaded, before = first_wait(dve, 16 * (b + 1), b)
                dve.wait_ge(x_loaded, loaded)
                if not isinstance(b, int) or b > 0:
                    dve.wait_ge(x_normed, before)
                    dve.wait_ge(rstd_done, before)
                moments(b, lambda n: xt[:, n * HALF:(n + 1) * HALF], 0, stats_done, mv_done)

            def norm_x(b):
                dve.wait_ge(rstd_done, b + 1)
                if not isinstance(b, int) or b > 0:
                    dve.wait_ge(q_proj, 2 * b)
                if not isinstance(b, int) or b > 2:
                    dve.wait_ge(xT_ready, 2 * (b - 2))
                nc.vector.tensor_scalar(xn[:, :], xt[:, :], mv[:, 0, 0:1], rstd[:, 0:1],
                                        ALU.subtract, ALU.mult).then_inc(x_normed, 1)

            def moments_row(b):
                whole, before = first_wait(dve, 2 * b + 2, b)
                dve.wait_ge(attended, whole)
                if not isinstance(b, int) or b > 0:
                    dve.wait_ge(row_normed, before)
                    dve.wait_ge(rstd2_done, before)
                moments(b, lambda n: rows[:, bass.ds(b, 1), n * HALF:(n + 1) * HALF].rearrange("p a t -> p (a t)"),
                        1, stats2_done, mv2_done)

            def norm_row(b, last):
                row = rows[:, bass.ds(b, 1), :].rearrange("p a t -> p (a t)")
                dve.wait_ge(rstd2_done, b + 1)
                dve.wait_ge(q_proj, 2 * B if last else 2 * b + 6)
                if not isinstance(b, int) or b > 0:
                    dve.wait_ge(xT_ready, 2 * b)
                nc.vector.tensor_scalar(xn[:, :], row, mv[:, 1, 0:1], rstd[:, 1:2],
                                        ALU.subtract, ALU.mult).then_inc(row_normed, 1)

            def soften(b, g):
                s = score[g % 2][:, 0:JQ * KW].rearrange("p (j k) -> p j k", k=KW)
                dve.wait_ge(scores_ready, G * b + g + 1)
                nc.vector.tensor_reduce(rmax[:, g % 2, :], s, AX.X, ALU.max).then_inc(max_ready, 1)
                dve.wait_ge(max_ready, G * b + g + 1)
                if not isinstance(b, int) or b > 0 or g >= 2:
                    dve.wait_ge(probs_turned, G * b + g - 1)
                    dve.wait_ge(sum_ready, G * b + g - 1)
                nc.vector.tensor_tensor(pr[:, g % 2, :, 0:KW], s,
                                        rmax[:, g % 2, :].unsqueeze(2).to_broadcast([P, JQ, KW]),
                                        ALU.subtract).then_inc(shifted, 1)

            def total(b, g):
                dve.wait_ge(probs_ready, G * b + g + 1)
                if g == 0 and (not isinstance(b, int) or b > 0):
                    dve.wait_ge(rinv_ready, b)
                nc.vector.tensor_reduce(rsum[:, g % 2, g // 2 * JQ:(g // 2 + 1) * JQ], pr[:, g % 2, :, 0:KW],
                                        AX.X, ALU.add).then_inc(sum_ready, 1)

            def pick(b, q):
                dve.wait_ge(pv_ready, G * b + 2 * q + 2)
                if q == 0 and (not isinstance(b, int) or b > 0):
                    dve.wait_ge(oT_ready, b)
                for h in range(2, HG):
                    for jj in range(2):
                        src = mixed[jj].rearrange("p (g j c) -> p g j c", g=2, c=GC)
                        lo = QB * h
                        last = nc.vector.tensor_copy(on[lo:lo + QB, :, q * PQ:(q + 1) * PQ, jj, :],
                                                     src[lo:lo + QB, :, :, HD * h:HD * h + HD])
                last.then_inc(picked_dve, 1)

            def invert(b):
                dve.wait_ge(sum_ready, G * b + G)
                if not isinstance(b, int) or b > 0:
                    dve.wait_ge(o_scaled, b)
                nc.vector.reciprocal(rinv[:, :], rsum[:, :, :].rearrange("p g j -> p (g j)")).then_inc(rinv_ready, 1)

            def turn_o(b):
                dve.wait_ge(picked_act, NQ * (b + 1))
                dve.wait_ge(picked_dve, NQ * (b + 1))
                dve.wait_ge(rinv_ready, b + 1)
                o = on[:, :, :, :, :].rearrange("p g j a d -> p (g j a) d")
                nc.vector.tensor_tensor(o, o, rinv[:, :].unsqueeze(2).to_broadcast([P, 2 * NJ, HD]), ALU.mult)\
                    .then_inc(o_scaled, 1)
                dve.wait_ge(o_scaled, b + 1)
                dve.wait_ge(v_placed, 112 * (min(b + 2, B) if isinstance(b, int) else b + 2))
                nc.vector.transpose(shared[:, 0:T],
                                    on[:, :, :, :, :].rearrange("p g j a d -> p (g j a d)")).then_inc(oT_ready, 1)

            def add_attention(b):
                dve.wait_ge(residual_set, b + 1)
                for jj in range(2):
                    dve.wait_ge(o_proj, 2 * b + jj + 1)
                    row = rows[:, bass.ds(b, 1), :].rearrange("p a (j e t) -> p (a j) e t", e=2, t=QB)[:, :, jj, :]
                    nc.vector.scalar_tensor_tensor(
                        out=row, in0=proj[jj].rearrange("p (j t) -> p j t", t=QB), scalar=tanh_g[:, 0:1],
                        in1=row, op0=ALU.mult, op1=ALU.add).then_inc(attended, 1)

            def take_xT(b):
                for n in range(2):
                    dve.wait_ge(hi_ready, 2 * b + n + 1)
                    hi = xT_hi[:, 4 * n:4 * n + 4, bass.ds(b * P, P)]
                    lo = xT_lo[:, 4 * n:4 * n + 4, bass.ds(b * P, P)]
                    nc.vector.scalar_tensor_tensor(out=lo, in0=proj[n].rearrange("p (k r) -> p k r", r=P), scalar=XS,
                                                   in1=hi, op0=ALU.mult, op1=ALU.subtract)\
                        .then_inc(lo_ready, 1)

            def take_v(b, n):
                dve.wait_ge(v_proj, 3 * b + n + 1)
                if n == 0 and (not isinstance(b, int) or b > 1):
                    dve.wait_ge(o_proj, 2 * b - 2)
                if n == 0 and (not isinstance(b, int) or b > 0):
                    dve.wait_ge(v_placed, 112 * b)
                if n < 2:
                    nc.vector.tensor_tensor(vn[:, 4 * n:4 * n + 4, :],
                                            proj[n].rearrange("p (n c) -> p n c", c=C),
                                            bv_all[:, :].unsqueeze(1).to_broadcast([P, 4, C]), ALU.add)\
                        .then_inc(v_ready, 1)
                else:
                    nc.vector.tensor_tensor(vn[0:WIN, 8, :], proj[0][0:WIN, 0:C], bv_all[0:WIN, :], ALU.add)\
                        .then_inc(v_ready, 1)

            moments_x(0)
            norm_x(0)
            dve.wait_ge(consts_loaded, 16 * N_CONST)
            for n in range(3):
                take_v(0, n)

            def batch(b, par, has_prev, has_next):
                for g in range(G):
                    soften(b, g)
                    if g > 0:
                        total(b, g - 1)
                    elif has_prev:
                        total(b - 1, G - 1)
                        invert(b - 1)
                    if g == 0 and has_next:
                        moments_x(b + 1)
                    if g == 1 and has_next:
                        norm_x(b + 1)
                    if g == 1 and has_prev:
                        pick(b - 1, 3)
                        turn_o(b - 1)
                    if g == 3 and has_prev:
                        add_attention(b - 1)
                    if g >= 3 and g % 2 == 1:
                        pick(b, (g - 3) // 2)
                    if g >= 5 and has_next:
                        take_v(b + 1, g - 5)
                    if g == 4 and has_prev:
                        moments_row(b - 1)
                    if g == 5 and has_prev:
                        norm_row(b - 1, not has_next)
                    if g == 7 and has_prev:
                        take_xT(b - 1)

            batches(dve, batch)
            total(B - 1, G - 1)
            invert(B - 1)
            pick(B - 1, 3)
            turn_o(B - 1)
            add_attention(B - 1)
            moments_row(B - 1)
            norm_row(B - 1, True)
            take_xT(B - 1)

            def scale_weight(c, n):
                slot = n % 2
                dve.wait_ge(zero_taken, c * NPC + n + 1)
                nc.vector.scalar_tensor_tensor(out=raw_s[:, slot].rearrange("p k i -> p (k i)"),
                                               in0=raw_z[:, slot].rearrange("p k i -> p (k i)"), scalar=WS,
                                               in1=raw_s[:, slot].rearrange("p k i -> p (k i)"),
                                               op0=ALU.mult, op1=ALU.mult).then_inc(scaled, 1)

            def hidden(c, t, i):
                u = (c * NT + t) * SC + i
                dve.wait_ge(up_ready, u + 1)
                dve.wait_ge(silu_ready, u + 1)
                if not isinstance(c, int) or c > 0 or t > 0 or i > 0:
                    dve.wait_ge(h_lo_ready, u)
                nc.vector.scalar_tensor_tensor(out=hid[:, :], in0=up_ps[i][:, :], scalar=1.0 / (XS * WS),
                                               in1=silu[:, :], op0=ALU.mult, op1=ALU.mult).then_inc(hid_ready, 1)
                dve.wait_ge(h_hi_ready, u + 1)
                nc.vector.tensor_tensor(h_lo[:, t % 2, i, :], hid[:, :], h_hi[:, t % 2, i, :], ALU.subtract)\
                    .then_inc(h_lo_ready, 1)

            def add_down(c, t):
                for r in range(TT):
                    n = (c * NT + t) * TT + r
                    dve.wait_ge(down_ready, n + 1)
                    if not isinstance(c, int) or c > 0:
                        dve.wait_ge(added, n - 2)
                    for half in range(2):
                        row = rows[:, t * TT + r, half * HALF:(half + 1) * HALF]
                        last = nc.vector.scalar_tensor_tensor(
                            out=row, in0=bank[4 + 2 * (r % 2) + half][:, :], scalar=ffn_gate[:, :], in1=row,
                            op0=ALU.mult, op1=ALU.add)
                    last.then_inc(added, 1)

            dve.wait_ge(scaled_bias, 3)
            for n in range(2 * SC):
                scale_weight(0, n)

            def one(c, par, first, last):
                for t in range(NT):
                    for i in range(SC):
                        hidden(c, t, i)
                    if t > 0:
                        add_down(c, t - 1)
                    elif not first:
                        add_down(c - 1, NT - 1)
                    if t == 0:
                        for i in range(SC):
                            scale_weight(c, 2 * SC + i)
                    if t in (1, 2) and not last:
                        for n in range(2 * (t - 1), 2 * t):
                            scale_weight(c + 1, n)

            passes(dve, one)
            add_down(NC - 1, NT - 1)

        @block.tensor
        def _(pe):
            pe.wait_ge(consts_loaded, 16 * N_CONST)
            pe.wait_ge(masks_made, 11)

            def bank_free(free):
                for s, count in free:
                    if not isinstance(count, int) or count > 0:
                        pe.wait_ge(s, count)

            def project_q(b, free):
                pe.wait_ge(x_normed, b + 1)
                for n in range(2):
                    bank_free(free(n))
                    nc.tensor.matmul(proj[n][:, :], wq[:, :], xn[:, n * HALF:(n + 1) * HALF],
                                     start=True, stop=True).then_inc(q_proj, 1)

            def project_k(b, free):
                pe.wait_ge(ctx_loaded, 16 * (b + 1))
                for n in range(2):
                    bank_free(free(n))
                    nc.tensor.matmul(proj[n][:, :], wk[:, :], ct[:, PAD + n * HALF:PAD + (n + 1) * HALF],
                                     start=True, stop=True).then_inc(k_proj, 1)

            def project_v(b, n, free):
                pe.wait_ge(ctx_loaded, 16 * (b + 1))
                bank_free(free)
                for j in range(4) if n < 2 else range(1):
                    start, m = (4 * n + j) * P, (P if n < 2 else QB)
                    last = nc.tensor.matmul(proj[n % 2][0:m, j * C:(j + 1) * C], ct[:, start:start + m], wv[:, :],
                                            start=True, stop=True)
                last.then_inc(v_proj, 1)

            def scores(b, g, par):
                q, hg = g // 2, g % 2
                if g == 0:
                    pe.wait_ge(k_ready, 2 * b + 2)
                if g == 0:
                    pe.wait_ge(q_spread, 2 * b + 1)
                if g == G // 2:
                    pe.wait_ge(q_spread, 2 * b + 2)
                if not isinstance(b, int) or b > 0 or g >= 2:
                    pe.wait_ge(shifted, G * b + g - 1)
                dst = score[g % 2][:, 0:JQ * KW].rearrange("p (j k) -> p j k", k=KW)
                lo = GC * hg
                nc.tensor.matmul(dst, spread[lo:lo + GC, :, :].rearrange("p h t -> p (h t)"),
                                 window[lo:lo + GC, :].unsqueeze(1).to_broadcast([GC, JQ, KW]),
                                 start=True, stop=False, skip_group_check=True)
                for j in range(JQ):
                    t = QB * (JQ * q + j)
                    last = nc.tensor.matmul(dst[:, j, :], qm[lo:lo + GC, JQ * q + j, :, :].rearrange("p h t -> p (h t)"), kt[lo:lo + GC, par, t:t + KW],
                                            start=False, stop=(j == JQ - 1), skip_group_check=True)
                last.then_inc(scores_ready, 1)

            def turn_probs(b, g):
                pe.wait_ge(probs_ready, G * b + g + 1)
                if not isinstance(b, int) or b > 0 or g >= 2:
                    pe.wait_ge(pT_ready, G * b + g - 1)
                for j in range(PQ):
                    last = nc.tensor.transpose(turned[g % 2][:, j * P:(j + 1) * P],
                                               pr[:, g % 2, 2 * j:2 * j + 2, :].rearrange("p a k -> p (a k)"),
                                               ident[:, :])
                last.then_inc(probs_turned, 1)

            def mix(b, g, par):
                q, hg = g // 2, g % 2
                pe.wait_ge(pT_ready, G * b + g + 1)
                if hg == 0:
                    pe.wait_ge(v_placed, 112 * (b + 1))
                    if not isinstance(b, int) or b > 0 or q > 0:
                        pe.wait_ge(picked_act, NQ * b + q)
                        pe.wait_ge(picked_dve, NQ * b + q)
                for j in range(PQ):
                    for jj in range(2):
                        lo = KP * jj
                        last = nc.tensor.matmul(mixed[jj][:, (hg * PQ + j) * GC:(hg * PQ + j + 1) * GC],
                                                pT[lo:lo + KW, g % 2, j * P:(j + 1) * P],
                                                vt[lo:lo + KW, par, q * PQ + j, hg * GC:(hg + 1) * GC],
                                                start=True, stop=True)
                last.then_inc(pv_ready, 1)

            def project_o(b, free):
                pe.wait_ge(oT_ready, b + 1)
                for jj in range(2):
                    bank_free(free(jj))
                    for hg in range(2):
                        last = nc.tensor.matmul(proj[jj][:, :], wo[:, hg, jj, :], oT[:, hg, :],
                                                start=(hg == 0), stop=(hg == 1))
                    last.then_inc(o_proj, 1)

            def turn_x(b, free):
                pe.wait_ge(row_normed, b + 1)
                for n in range(2):
                    bank_free(free(n))
                    for k in range(4):
                        f = (4 * n + k) * P
                        last = nc.tensor.transpose(proj[n][:, k * P:(k + 1) * P], xn[:, f:f + P], ident[:, :])
                    last.then_inc(xT_ready, 1)

            project_q(0, lambda n: [])
            project_k(0, lambda n: [(q_ready, n + 1)])
            project_v(0, 0, [(k_ready, 1)])
            project_v(0, 1, [(k_ready, 2)])
            project_v(0, 2, [(v_ready, 1)])

            def batch(b, par, has_prev, has_next):
                for g in range(G):
                    scores(b, g, par)
                    if g > 0:
                        turn_probs(b, g - 1)
                    elif has_prev:
                        turn_probs(b - 1, G - 1)
                    if g > 1:
                        mix(b, g - 2, par)
                    elif has_prev:
                        mix(b - 1, G - 2 + g, 1 - par)
                    if g == 2 and has_next:
                        project_q(b + 1, lambda n: [(v_ready, 3 * b + 3)] + [(lo_ready, 2 * b - 2)] * has_prev)
                    if g == 3 and has_prev:
                        project_o(b - 1, (lambda n: [(q_ready, 2 * b + n + 3)]) if has_next else
                                  (lambda n: [(lo_ready, 2 * b - 2)]))
                    if g == 4 and has_next:
                        project_k(b + 1, (lambda n: [(attended, 2 * b + n - 1)]) if has_prev else
                                  (lambda n: [(q_ready, n + 3)]))
                    if g in (5, 6) and has_next:
                        project_v(b + 1, g - 5, [(k_ready, 2 * b + g - 2)])
                    if g == 7:
                        if has_next:
                            project_v(b + 1, 2, [(v_ready, 3 * b + 4)])
                        if has_prev:
                            turn_x(b - 1, (lambda n: [(v_ready, 3 * b + 6)]) if has_next else
                                   (lambda n: [(attended, 2 * b)]))

            batches(pe, batch)
            turn_probs(B - 1, G - 1)
            mix(B - 1, G - 2, 1)
            mix(B - 1, G - 1, 1)
            project_o(B - 1, lambda n: [(lo_ready, 2 * B - 2)])
            turn_x(B - 1, lambda n: [(attended, 2 * B)])

            pe.wait_ge(lo_ready, 2 * B)

            def gate_up(c, t, par):
                for i in range(SC):
                    u = (c * NT + t) * SC + i
                    for m, (ps, ready) in enumerate(((gate_ps, gate_ready), (up_ps, up_ready))):
                        if t == 0:
                            pe.wait_ge(w_lo_ready, c * NPC + 2 * i + m + 1)
                        if not isinstance(c, int) or c > 0 or t > 0:
                            pe.wait_ge((silu_ready, hid_ready)[m], u - 1)
                        for k in range(NK):
                            hi, lo = w_hi[:, par, i, m, k, :], w_lo[:, par, i, m, k, :]
                            xh, xl = xT_hi[:, k, t * TB:(t + 1) * TB], xT_lo[:, k, t * TB:(t + 1) * TB]
                            nc.tensor.matmul(ps[i][:, :], hi, xh, start=(k == 0), stop=False)
                            nc.tensor.matmul(ps[i][:, :], hi, xl, start=False, stop=False)
                            last = nc.tensor.matmul(ps[i][:, :], lo, xh, start=False, stop=(k == NK - 1))
                        last.then_inc(ready, 1)

            def down(c, t, par):
                pe.wait_ge(h_lo_ready, (c * NT + t + 1) * SC)
                if t == 0:
                    pe.wait_ge(w_lo_ready, (c + 1) * NPC)
                for r in range(TT):
                    n = (c * NT + t) * TT + r
                    if not isinstance(c, int) or c > 0 or t > 0 or r > 1:
                        pe.wait_ge(added, n - 1)
                    for half in range(2):
                        ps = bank[4 + 2 * (r % 2) + half]
                        for i in range(SC):
                            hh, hl = h_hi[:, t % 2, i, r * P:(r + 1) * P], h_lo[:, t % 2, i, r * P:(r + 1) * P]
                            dh = d_hi[:, i, half * HALF:(half + 1) * HALF]
                            dl = d_lo[:, i, half * HALF:(half + 1) * HALF]
                            nc.tensor.matmul(ps[:, :], hh, dh, start=(i == 0), stop=False)
                            nc.tensor.matmul(ps[:, :], hh, dl, start=False, stop=False)
                            last = nc.tensor.matmul(ps[:, :], hl, dh, start=False, stop=(i == SC - 1))
                    last.then_inc(down_ready, 1)

            def one(c, par, first, last):
                for t in range(NT):
                    gate_up(c, t, par)
                    if t > 0:
                        down(c, t - 1, par)
                    elif not first:
                        down(c - 1, NT - 1, par)

            passes(pe, one)
            down(NC - 1, NT - 1, 1)


_INS = ['x', 'ctx_4096', 'g_xattn', 'g_ffn', 'L0_xattn_Wq', 'L0_xattn_bq', 'L0_xattn_Wk', 'L0_xattn_bk',
        'L0_xattn_Wv', 'L0_xattn_bv', 'L0_xattn_Wo', 'L0_xattn_bo', 'L0_ffn_gate_w', 'L0_ffn_gate_z',
        'L0_ffn_gate_s', 'L0_ffn_up_w', 'L0_ffn_up_z', 'L0_ffn_up_s', 'L0_ffn_down_w', 'L0_ffn_down_z',
        'L0_ffn_down_s']
_TRANSPOSED = ('L0_xattn_Wq', 'L0_xattn_Wk', 'L0_xattn_Wv', 'L0_xattn_Wo')


def kernel(**inputs):
    import numpy as _np
    import concourse.bacc as _bacc
    from concourse import mybir as _mybir
    from concourse.bass_utils import run_bass_kernel_spmd as _run

    nc = _bacc.Bacc("TRN2", target_bir_lowering=False, num_devices=1)
    arrays, args = {}, []
    for name in _INS:
        a = _np.asarray(inputs[name])
        a = _np.ascontiguousarray(a.T if name in _TRANSPOSED else a)
        arrays[f"in_{name}_dram"] = a
        args.append(nc.dram_tensor(f"in_{name}_dram", a.shape, _mybir.dt.from_np(a.dtype), kind="ExternalInput").ap())
    args.append(nc.dram_tensor("out_0_dram", (16, 128, 1024), _mybir.dt.float32, kind="ExternalOutput").ap())
    flamingo_layer(nc, *args)
    r = _run(nc, [arrays], core_ids=[0])
    return r.results[0]["out_0_dram"]
```

```python
import concourse.bass as bass
from concourse import mybir
from contextlib import ExitStack


def flamingo_layer(nc, x_in, ctx_in, g_xattn, g_ffn, WqT, bq, WkT, bk, WvT, bv, WoT, bo,
                   gate_w, gate_z, gate_s, up_w, up_z, up_s, down_w, down_z, down_s, out):
    fp32, fp16, bf16, i32 = mybir.dt.float32, mybir.dt.float16, mybir.dt.bfloat16, mybir.dt.int32
    ALU, ACT, AX = mybir.AluOpType, mybir.ActivationFunctionType, mybir.AxisListType
    P = 128

    B, C, T = x_in.shape
    HEADS, WIN = 8, 16
    HD = C // HEADS
    PAD = WIN // 2
    QB = 32
    KW = QB + WIN
    KP = 64
    NJ = T // QB
    HG = 4
    GC = HG * HD
    NQ = 4
    JQ = NJ // NQ
    G = NQ * 2
    HALF = 512
    EPS = 1e-5
    MASKED = -1e30

    F = gate_w.shape[1]
    NK = T // P
    SC = 2
    NC = F // (P * SC)
    ROWS = B * C
    TB = 512
    NT = ROWS // TB
    TT = TB // P
    XS = 256.0
    WS = 4096.0
    NPC = 3 * SC

    ctx = ExitStack()
    with ctx:
        def sb(name, shape, dt, stack=ctx):
            return stack.enter_context(nc.sbuf_tensor(name, shape, dt))

        def sem(name):
            return ctx.enter_context(nc.semaphore(name))

        rows = sb("rows", [P, B, T], fp32)
        gates = sb("gates", [P, 2], fp32)
        tanh_g = sb("tanh_g", [P, 2], fp32)
        ffn_gate = sb("ffn_gate", [P, 1], fp32)

        att = ExitStack()
        wq = sb("wq", [P, C], fp32, att)
        wk = sb("wk", [P, C], fp32, att)
        wv = sb("wv", [P, C], fp32, att)
        wo = sb("wo", [P, 2, 2, C], fp32, att)
        bias = sb("bias", [P, 3], fp32, att)
        bo_g = sb("bo_g", [P, 1], fp32, att)
        bv_all = sb("bv_all", [P, C], fp32, att)
        CW = PAD + T + 24
        head_of = sb("head_of", [P, HG], fp32, att)
        ident = sb("ident", [P, P], fp32, att)
        ident16 = sb("ident16", [P, P], fp16, att)
        spread = sb("spread", [P, HG, QB], bf16, att)
        window = sb("window", [P, KW], bf16, att)
        xt = sb("xt", [P, T], fp32, att)
        ct = sb("ct", [P, CW], fp32, att)
        xn = sb("xn", [P, T], fp32, att)
        stats = sb("stats", [P, 2, 2, 6], fp32, att)
        mv = sb("mv", [P, 2, 2], fp32, att)
        var_eps = sb("var_eps", [P, 2], fp32, att)
        minus_half = sb("minus_half", [P, 1], fp32, att)
        rstd = sb("rstd", [P, 2], fp32, att)
        nat = sb("nat", [P, T], fp32, att)
        k_hl = sb("k_hl", [P, 2, T], fp16, att)
        q_hl = sb("q_hl", [P, 2, T], fp16, att)
        qs = sb("qs", [P, 2, T], fp16, att)
        qm = sb("qm", [P, 2, NJ, HG, QB], fp16, att)
        ks = sb("ks", [P, 2, 2, 2, T + WIN], fp16, att)
        vn = sb("vn", [P, 9, C], fp32, att)
        vn_hl = sb("vn_hl", [P, 9, 2, C], fp16, att)
        vt = sb("vt", [P, 2, NJ, 2, C], fp16, att)
        pr = sb("pr", [P, 2, JQ, KW], fp32, att)
        NP = 4
        p_hl = sb("p_hl", [P, NP, JQ, 2, KP], fp16, att)
        pT = sb("pT", [P, 2, JQ * P], fp16, att)
        rmax = sb("rmax", [P, 2, JQ], fp32, att)
        rsum = sb("rsum", [P, 2, NJ], fp32, att)
        rinv = sb("rinv", [P, 2 * NJ], fp32, att)
        on = sb("on", [P, 2, NJ, HD], fp32, att)
        oT = sb("oT", [P, 2, HALF], fp32, att)
        xs = sb("xs", [P, 2, NK, P], fp16, att)
        att.close()

        w_hi = sb("w_hi", [P, 2, SC, 2, NK, P], fp16)
        w_lo = sb("w_lo", [P, 2, SC, 2, NK, P], fp16)
        d_hi = sb("d_hi", [P, SC, T], fp16)
        d_lo = sb("d_lo", [P, SC, T], fp16)
        raw_w = sb("raw_w", [P, 2, NK, P], i32)
        raw_z = sb("raw_z", [P, 2, NK, P], i32)
        raw_s = sb("raw_s", [P, 2, NK, P], fp32)
        silu = sb("silu", [P, TB], fp32)
        hid = sb("hid", [P, TB], fp32)
        h_hi = sb("h_hi", [P, 2, SC, TB], fp16)
        h_lo = sb("h_lo", [P, 2, SC, TB], fp16)
        xT = sb("xT", [P, B, 2, NK, P], fp16)
        xT_dram = nc.dram_tensor("xT_spill", (B, P, 2 * NK * P), fp16, kind="Internal").ap()

        bank = [ctx.enter_context(nc.psum_tensor(f"bank{n}", [P, HALF], fp32)) for n in range(8)]
        proj = bank[0:2]
        score = bank[2:4]
        turned = [ctx_t[:, :].bitcast(fp16) for ctx_t in bank[4:6]]
        mixed = bank[6:8]
        gate_ps = bank[0:2]
        up_ps = bank[2:4]

        consts_loaded, gates_loaded = sem("consts_loaded"), sem("gates_loaded")
        zeroed, consts_made, masks_made, gates_ready, scaled_bias = (
            sem("zeroed"), sem("consts_made"), sem("masks_made"), sem("gates_ready"), sem("scaled_bias"))
        x_loaded, ctx_loaded, q_moved, k_moved, v_placed, q_spread = (
            sem("x_loaded"), sem("ctx_loaded"), sem("q_moved"), sem("k_moved"), sem("v_placed"), sem("q_spread"))
        residual_set = sem("residual_set")
        eps_added = [sem("eps_added"), sem("eps2_added")]
        stats_done, mv_done, rstd_done, x_normed = sem("stats_done"), sem("mv_done"), sem("rstd_done"), sem("x_normed")
        q_proj, k_proj, v_proj, o_proj, xT_ready = (
            sem("q_proj"), sem("k_proj"), sem("v_proj"), sem("o_proj"), sem("xT_ready"))
        q_nat, k_nat, v_nat = sem("q_nat"), sem("k_nat"), sem("v_nat")
        q_hi, k_hi, v_hi, p_hi = sem("q_hi"), sem("k_hi"), sem("v_hi"), sem("p_hi")
        q_lo, k_lo, v_lo, p_lo = sem("q_lo"), sem("k_lo"), sem("v_lo"), sem("p_lo")
        scores_ready, max_ready, shifted, probs_ready, sum_ready = (
            sem("scores_ready"), sem("max_ready"), sem("shifted"), sem("probs_ready"), sem("sum_ready"))
        probs_turned, pT_ready, pv_ready = sem("probs_turned"), sem("pT_ready"), sem("pv_ready")
        picked_act, picked_dve = sem("picked_act"), sem("picked_dve")
        rinv_ready, o_scaled, oT_ready, attended = (
            sem("rinv_ready"), sem("o_scaled"), sem("oT_ready"), sem("attended"))
        stats2_done, mv2_done, rstd2_done, row_normed = (
            sem("stats2_done"), sem("mv2_done"), sem("rstd2_done"), sem("row_normed"))
        hi_ready, lo_ready, spilled, vn_zeroed = sem("hi_ready"), sem("lo_ready"), sem("spilled"), sem("vn_zeroed")
        xT_loaded = [sem(f"xT_block{t}_loaded") for t in range(NT)]

        raw_loaded = [sem("raw0_loaded"), sem("raw1_loaded")]
        zero_taken, scaled, w_hi_ready, w_lo_ready = (
            sem("zero_taken"), sem("scaled"), sem("w_hi_ready"), sem("w_lo_ready"))
        gate_ready, up_ready, silu_ready, hid_ready, h_hi_ready, h_lo_ready = (
            sem("gate_ready"), sem("up_ready"), sem("silu_ready"), sem("hid_ready"), sem("h_hi_ready"),
            sem("h_lo_ready"))
        down_ready, added = sem("down_ready"), sem("added")
        stored = sem("stored")

        N_CONST = 7 + 16

        def batches(eng, batch):
            batch(0, 0, 0, 2)
            batch(1, 1, 1, 2)
            with eng.Fori(1, B // 2 - 1) as i:
                batch(2 * i, 0, 2, 2)
                batch(2 * i + 1, 1, 2, 2)
            batch(B - 2, 0, 2, 1)
            batch(B - 1, 1, 2, 0)

        def lag(b, g, n, prev):
            if g >= n:
                return [(b, g - n)]
            return [(b - 1, G + g - n)] if prev else []

        def passes(eng, one):
            one(0, 0, True, False)
            with eng.Fori(0, (NC - 2) // 2) as i:
                one(2 * i + 1, 1, False, False)
                one(2 * i + 2, 0, False, False)
            one(NC - 1, 1, False, True)

        def first_wait(eng, *values):
            values = [v if isinstance(v, int) else eng.snap(eng.to_reg(v)) for v in values]
            eng.wait_ge(consts_made, 5)
            return values

        block = ctx.enter_context(nc.Block())

        @block.sync
        def _(sp):
            sp.dma_start(xt[:, :], x_in[0]).then_inc(x_loaded, 16)
            sp.dma_start(wq[:, :], WqT).then_inc(consts_loaded, 16)
            sp.dma_start(wk[:, :], WkT).then_inc(consts_loaded, 16)
            sp.dma_start(wv[:, :], WvT).then_inc(consts_loaded, 16)
            for n, v in enumerate((bq, bk, bo)):
                sp.dma_start(bias[:, n:n + 1], v.rearrange("(p a) -> p a", a=1)).then_inc(consts_loaded, 16)
            sp.dma_start(bv_all[:, :], bv.partition_broadcast(P)).then_inc(consts_loaded, 16)
            for n, v in enumerate((g_xattn, g_ffn)):
                sp.dma_start(gates[:, n:n + 1], v.partition_broadcast(P)).then_inc(gates_loaded, 16)
            sp.wait_ge(zeroed, 2)
            sp.dma_start(ct[:, PAD:PAD + T], ctx_in[0]).then_inc(ctx_loaded, 16)
            for h in range(HG):
                for hg in range(2):
                    for jj in range(2):
                        lo = QB * h + HD * jj
                        src = HD * (HG * hg + h)
                        sp.dma_start(wo[lo:lo + HD, hg, jj, :], WoT[src:src + HD, :])\
                          .then_inc(consts_loaded, 16)

            def load_x(b):
                used, = first_wait(sp, b)
                if not isinstance(b, int) or b > 0:
                    sp.wait_ge(x_normed, used)
                    sp.wait_ge(residual_set, used)
                sp.dma_start(xt[:, :], x_in[bass.ds(b, 1)].rearrange("a c t -> (a c) t")).then_inc(x_loaded, 16)

            def load_ctx(b):
                used, = first_wait(sp, 3 * b)
                sp.wait_ge(v_proj, used)
                sp.dma_start(ct[:, PAD:PAD + T], ctx_in[bass.ds(b, 1)].rearrange("a c t -> (a c) t"))\
                  .then_inc(ctx_loaded, 16)

            def move_k(b, par):
                ready, used = first_wait(sp, b + 1, G * (b - 1))
                sp.wait_ge(k_lo, ready)
                if not isinstance(b, int) or b > 1:
                    sp.wait_ge(scores_ready, used)
                for hg in range(2):
                    for copy in range(2):
                        sp.dma_start(ks[GC * copy:GC * copy + GC, par, hg, :, PAD:PAD + T],
                                     k_hl[GC * hg:GC * hg + GC, :, :]).then_inc(k_moved, 16)

            def move_q(b):
                ready, used = first_wait(sp, b + 1, 2 * b)
                sp.wait_ge(q_lo, ready)
                if not isinstance(b, int) or b > 0:
                    sp.wait_ge(q_spread, used)
                for hg in range(2):
                    for part in range(2):
                        sp.dma_start(qs[GC * part:GC * part + GC, hg, :],
                                     q_hl[GC * hg:GC * hg + GC, part, :]).then_inc(q_moved, 16)

            def place_v(b, par):
                ready, used = first_wait(sp, b + 1, G * (b - 1))
                sp.wait_ge(v_lo, ready)
                if not isinstance(b, int) or b > 1:
                    sp.wait_ge(pv_ready, used)
                for d in (0, KP):
                    for dst, src in (
                            (vt[d + PAD:d + KW, par, 0], vn_hl[PAD:KW, 0]),
                            (vt[d:d + KW, par, 4:NJ:4], vn_hl[0:KW, 1:8]),
                            (vt[d:d + KW, par, 1:NJ:4], vn_hl[QB:QB + KW, 0:8]),
                            (vt[d:d + KW, par, 2:NJ:4], vn_hl[2 * QB:2 * QB + KW, 0:8]),
                            (vt[d:d + QB, par, 3:NJ:4], vn_hl[3 * QB:P, 0:8]),
                            (vt[d + QB:d + KW, par, 3:NJ - 1:4], vn_hl[0:WIN, 1:8]),
                            (vt[d + QB:d + QB + PAD, par, NJ - 1], vn_hl[0:PAD, 8])):
                        sp.dma_start(dst, src).then_inc(v_placed, 16)

            def spill(b):
                done, = first_wait(sp, 2 * b + 2)
                sp.wait_ge(lo_ready, done)
                sp.dma_start(xT_dram[bass.ds(b, 1)].rearrange("a p n -> (a p) n"),
                             xs[:, :, :, :].rearrange("p h k r -> p (h k r)")).then_inc(spilled, 16)

            sp.wait_ge(zeroed, 5)
            move_k(0, 0)
            load_x(1)
            load_ctx(1)
            move_q(0)
            place_v(0, 0)

            def batch(b, par, prev, next):
                if prev >= 2:
                    spill(b - 2)
                if next >= 2:
                    load_x(b + 2)
                if next:
                    move_k(b + 1, 1 - par)
                if next >= 2:
                    load_ctx(b + 2)
                if next:
                    move_q(b + 1)
                    place_v(b + 1, 1 - par)

            batches(sp, batch)
            spill(B - 2)
            spill(B - 1)
            sp.wait_ge(spilled, 16 * B)
            for b in range(B):
                sp.dma_start(xT[:, b].rearrange("p h k r -> p (h k r)"), xT_dram[b]).then_inc(xT_loaded[b // TT], 16)

            def load_piece(c, n, first):
                slot = n % 2
                if first:
                    if slot == 0 and n == 0:
                        sp.wait_ge(spilled, 16 * B)
                used, = first_wait(sp, NPC * c + n - 1)
                if not (first and n < 2):
                    sp.wait_ge(w_lo_ready, used)
                w, z, s = raw_w[:, slot], raw_z[:, slot], raw_s[:, slot]
                if n < 2 * SC:
                    ww, zz, ss = ((gate_w, gate_z, gate_s), (up_w, up_z, up_s))[n % 2]
                    col = (c * SC + n // 2) * P
                    src = ww[:, bass.ds(col, P)].rearrange("(k p) i -> p k i", p=P)
                    zrc = zz[:, bass.ds(col, P)].partition_broadcast(P)
                    src_s = ss[:, bass.ds(col, P)].partition_broadcast(P)
                else:
                    r = c * SC + n - 2 * SC
                    src = down_w[bass.ds(r * P, P), :].rearrange("p (k i) -> p k i", k=NK)
                    zrc = down_z[bass.ds(r, 1), :].rearrange("a (k i) -> (a k) i", k=NK).partition_broadcast(P)
                    src_s = down_s[bass.ds(r, 1), :].rearrange("a (k i) -> (a k) i", k=NK).partition_broadcast(P)
                sp.dma_start(w, src).then_inc(raw_loaded[slot], 16)
                sp.dma_start(z, zrc).then_inc(raw_loaded[slot], 16)
                sp.dma_start(s, src_s).then_inc(raw_loaded[slot], 16)

            for n in range(2 * SC):
                load_piece(0, n, True)

            def one(c, par, first, last):
                for n in range(2 * SC, NPC):
                    load_piece(c, n, False)
                if not last:
                    for n in range(2 * SC):
                        load_piece(c + 1, n, False)

            passes(sp, one)

            for t in range(B):
                sp.wait_ge(added, (NC - 1) * B + t + 1)
                sp.dma_start(out[t], rows[:, t, :]).then_inc(stored, 16)
            sp.wait_ge(stored, 16 * B)

        @block.gpsimd
        def _(pool):
            nc.gpsimd.memset(ct[:, :], 0.0).then_inc(zeroed, 1)
            nc.gpsimd.memset(wo[:, :, :, :], 0.0).then_inc(zeroed, 1)
            nc.gpsimd.memset(vt[:, :, :, :, :], 0.0).then_inc(zeroed, 1)
            nc.gpsimd.memset(ks[:, :, :, :, :], 0.0).then_inc(zeroed, 1)
            nc.gpsimd.memset(p_hl[:, :, :, :, :], 0.0).then_inc(zeroed, 1)
            nc.gpsimd.memset(head_of[:, :], 1.0).then_inc(consts_made, 1)
            nc.gpsimd.memset(minus_half[:, :], -0.5).then_inc(consts_made, 1)
            nc.gpsimd.memset(ident[:, :], 0.0).then_inc(consts_made, 1)
            nc.gpsimd.memset(spread[:, :, :], 0.0).then_inc(consts_made, 1)
            nc.gpsimd.memset(window[:, :], 0.0).then_inc(consts_made, 1)
            pool.wait_ge(consts_made, 5)
            nc.gpsimd.affine_select(out=ident[:, :], in_=ident[:, :], compare_op=ALU.not_equal, fill=1.0,
                                    base=0, pattern=[[-1, P]], channel_multiplier=1).then_inc(masks_made, 1)
            sp_rows, win = spread[0:QB, :, :], window[0:QB, :]
            nc.gpsimd.affine_select(out=sp_rows, in_=sp_rows, compare_op=ALU.not_equal, fill=1.0, base=0,
                                    pattern=[[0, HG], [-1, QB]], channel_multiplier=1).then_inc(masks_made, 1)
            nc.gpsimd.affine_select(out=win, in_=win, compare_op=ALU.is_ge, fill=MASKED, base=0,
                                    pattern=[[1, KW]], channel_multiplier=-1).then_inc(masks_made, 1)
            pool.wait_ge(masks_made, 3)
            nc.gpsimd.affine_select(out=win, in_=win, compare_op=ALU.is_ge, fill=MASKED, base=WIN - 1,
                                    pattern=[[-1, KW]], channel_multiplier=1).then_inc(masks_made, 1)
            nc.gpsimd.tensor_copy(ident16[:, :], ident[:, :]).then_inc(masks_made, 1)
            for n, lo in enumerate((0, GC)):
                mine = head_of[lo:lo + GC, :]
                nc.gpsimd.affine_select(out=mine, in_=mine, compare_op=ALU.is_ge, fill=0.0, base=0,
                                        pattern=[[-HD, HG]], channel_multiplier=1).then_inc(masks_made, 1)
                pool.wait_ge(masks_made, 6 + 2 * n)
                nc.gpsimd.affine_select(out=mine, in_=mine, compare_op=ALU.is_ge, fill=0.0, base=HD - 1,
                                        pattern=[[HD, HG]], channel_multiplier=-1).then_inc(masks_made, 1)

            pool.wait_ge(masks_made, 9)

            def inverse_std(b, which, moments_ready, used, done):
                now, before = first_wait(pool, b + 1, b)
                pool.wait_ge(moments_ready, now)
                if not isinstance(b, int) or b > 0:
                    pool.wait_ge(used, before)
                nc.gpsimd.tensor_scalar(var_eps[:, which:which + 1], mv[:, which, 1:2], EPS, None, ALU.add)\
                    .then_inc(eps_added[which], 1)
                pool.wait_ge(eps_added[which], b + 1)
                nc.gpsimd.tensor_tensor(rstd[:, which:which + 1], var_eps[:, which:which + 1], minus_half[:, :],
                                        ALU.pow)\
                    .then_inc(done, 1)

            def low_k(b):
                pool.wait_ge(k_hi, b + 1)
                nc.gpsimd.tensor_tensor(k_hl[:, 1, :], nat[:, :], k_hl[:, 0, :], ALU.subtract).then_inc(k_lo, 1)

            def low_q(b):
                pool.wait_ge(q_hi, b + 1)
                nc.gpsimd.tensor_tensor(q_hl[:, 1, :], nat[:, :], q_hl[:, 0, :], ALU.subtract).then_inc(q_lo, 1)

            def low_v(b):
                pool.wait_ge(v_hi, b + 1)
                nc.gpsimd.tensor_tensor(vn_hl[:, :, 1, :], vn[:, :, :], vn_hl[:, :, 0, :], ALU.subtract)\
                    .then_inc(v_lo, 1)

            def low_p(b, g):
                n, = first_wait(pool, G * b + g + 1)
                pool.wait_ge(p_hi, n)
                nc.gpsimd.tensor_tensor(p_hl[:, g % NP, :, 1, 0:KW], pr[:, g % 2], p_hl[:, g % NP, :, 0, 0:KW],
                                        ALU.subtract).then_inc(p_lo, 1)

            inverse_std(0, 0, mv_done, x_normed, rstd_done)
            low_k(0)
            low_q(0)
            low_v(0)

            def batch(b, par, prev, next):
                for g in range(G):
                    if g == 6 and prev:
                        inverse_std(b - 1, 1, mv2_done, row_normed, rstd2_done)
                    low_p(b, g)
                    if g == 0 and next:
                        inverse_std(b + 1, 0, mv_done, x_normed, rstd_done)
                    if g == 3 and next:
                        low_k(b + 1)
                    if g == 4 and next:
                        low_q(b + 1)
                    if g == 5 and next:
                        low_v(b + 1)

            batches(pool, batch)
            inverse_std(B - 1, 1, mv2_done, row_normed, rstd2_done)

            def take_zero(c, n):
                slot = n % 2
                pool.wait_ge(raw_loaded[slot], (c * (NPC // 2) + n // 2 + 1) * 48)
                nc.gpsimd.tensor_tensor(raw_z[:, slot], raw_w[:, slot], raw_z[:, slot], ALU.subtract)\
                    .then_inc(zero_taken, 1)

            def low_weight(c, n, par):
                slot = n % 2
                pool.wait_ge(w_hi_ready, c * NPC + n + 1)
                if n < 2 * SC:
                    hi = w_hi[:, par, n // 2, n % 2].rearrange("p k i -> p (k i)")
                    lo = w_lo[:, par, n // 2, n % 2].rearrange("p k i -> p (k i)")
                else:
                    hi, lo = d_hi[:, n - 2 * SC, :], d_lo[:, n - 2 * SC, :]
                nc.gpsimd.tensor_tensor(lo, raw_s[:, slot].rearrange("p k i -> p (k i)"), hi, ALU.subtract)\
                    .then_inc(w_lo_ready, 1)

            take_zero(0, 0)
            for n in range(1, 2 * SC):
                take_zero(0, n)
                low_weight(0, n - 1, 0)

            def one(c, par, first, last):
                for n in range(2 * SC, NPC):
                    take_zero(c, n)
                    low_weight(c, n - 1, par)
                if last:
                    low_weight(c, NPC - 1, par)
                else:
                    take_zero(c + 1, 0)
                    low_weight(c, NPC - 1, par)
                    for n in range(1, 2 * SC):
                        take_zero(c + 1, n)
                        low_weight(c + 1, n - 1, 1 - par)

            passes(pool, one)

        @block.scalar
        def _(act):
            act.wait_ge(gates_loaded, 32)
            nc.scalar.activation(tanh_g[:, :], gates[:, :], ACT.Tanh).then_inc(gates_ready, 1)
            act.wait_ge(gates_ready, 1)
            nc.scalar.activation(ffn_gate[:, :], tanh_g[:, 1:2], ACT.Copy, scale=1.0 / WS).then_inc(scaled_bias, 1)
            act.wait_ge(consts_loaded, 16 * N_CONST)
            nc.scalar.activation(bo_g[:, :], bias[:, 2:3], ACT.Identity, scale=tanh_g[:, 0:1]).then_inc(scaled_bias, 1)
            act.wait_ge(scaled_bias, 2)
            act.wait_ge(zeroed, 5)

            def set_residual(b):
                act.wait_ge(x_loaded, 16 * (b + 1))
                nc.scalar.activation(rows[:, bass.ds(b, 1), :].rearrange("p a t -> p (a t)"), xt[:, :], ACT.Identity,
                                     bias=bo_g[:, :]).then_inc(residual_set, 1)

            def take_k(b):
                for n in range(2):
                    act.wait_ge(k_proj, 2 * b + n + 1)
                    if n == 0 and (not isinstance(b, int) or b > 0):
                        act.wait_ge(q_lo, b)
                    nc.scalar.activation(nat[:, n * HALF:(n + 1) * HALF], proj[n][:, :], ACT.Identity,
                                         bias=bias[:, 1:2]).then_inc(k_nat, 1)
                act.wait_ge(k_nat, 2 * b + 2)
                if not isinstance(b, int) or b > 0:
                    act.wait_ge(k_moved, 64 * b)
                nc.scalar.activation(k_hl[:, 0, :], nat[:, :], ACT.Copy).then_inc(k_hi, 1)

            def take_q(b):
                for n in range(2):
                    act.wait_ge(q_proj, 2 * b + n + 1)
                    if n == 0:
                        act.wait_ge(k_lo, b + 1)
                    nc.scalar.activation(nat[:, n * HALF:(n + 1) * HALF], proj[n][:, :], ACT.Identity,
                                         bias=bias[:, 0:1]).then_inc(q_nat, 1)
                act.wait_ge(q_nat, 2 * b + 2)
                if not isinstance(b, int) or b > 0:
                    act.wait_ge(q_moved, 64 * b)
                nc.scalar.activation(q_hl[:, 0, :], nat[:, :], ACT.Copy).then_inc(q_hi, 1)

            def high_v(b):
                act.wait_ge(v_nat, 3 * b + 3)
                if not isinstance(b, int) or b > 0:
                    act.wait_ge(v_placed, 224 * b)
                nc.scalar.activation(vn_hl[:, :, 0, :], vn[:, :, :], ACT.Copy).then_inc(v_hi, 1)

            def exp(b, g):
                act.wait_ge(shifted, G * b + g + 1)
                nc.scalar.activation(pr[:, g % 2], pr[:, g % 2], ACT.Exp, scale=HD ** -0.5)\
                    .then_inc(probs_ready, 1)
                act.wait_ge(probs_ready, G * b + g + 1)
                if not isinstance(b, int) or b > 0 or g >= NP:
                    act.wait_ge(probs_turned, G * b + g + 1 - NP)
                nc.scalar.activation(p_hl[:, g % NP, :, 0, 0:KW], pr[:, g % 2], ACT.Copy).then_inc(p_hi, 1)

            def take_pT(b, g):
                act.wait_ge(probs_turned, G * b + g + 1)
                if not isinstance(b, int) or b > 0 or g >= 2:
                    act.wait_ge(pv_ready, G * b + g - 1)
                nc.scalar.activation(pT[:, g % 2, :], turned[g % 2], ACT.Copy).then_inc(pT_ready, 1)

            def pick(b, g):
                q, hg = g // 2, g % 2
                act.wait_ge(pv_ready, G * b + g + 1)
                if g == 0 and (not isinstance(b, int) or b > 0):
                    act.wait_ge(oT_ready, b)
                src = mixed[g % 2].rearrange("p (j c) -> p j c", c=GC)
                for h in range(2):
                    lo = QB * h
                    last = nc.scalar.activation(on[lo:lo + QB, hg, q * JQ:(q + 1) * JQ, :],
                                                src[lo:lo + QB, :, HD * h:HD * h + HD], ACT.Copy)
                last.then_inc(picked_act, 1)

            def take_xT(b):
                for n in range(2):
                    act.wait_ge(xT_ready, 2 * b + n + 1)
                    if n == 0 and (not isinstance(b, int) or b > 0):
                        act.wait_ge(spilled, 16 * b)
                    nc.scalar.activation(xs[:, 0, 4 * n:4 * n + 4, :].rearrange("p k r -> p (k r)"), proj[n][:, :],
                                         ACT.Copy, scale=XS).then_inc(hi_ready, 1)

            set_residual(0)
            take_k(0)
            take_q(0)
            high_v(0)

            def batch(b, par, prev, next):
                for g in range(G):
                    exp(b, g)
                    for at in lag(b, g, 2, prev):
                        take_pT(*at)
                    for at in lag(b, g, 4, prev):
                        pick(*at)
                    if g == 0 and prev >= 2:
                        take_xT(b - 2)
                    if g == 0 and next:
                        set_residual(b + 1)
                    if g == 2 and next:
                        take_k(b + 1)
                    if g == 3 and next:
                        take_q(b + 1)
                    if g == 5 and next:
                        high_v(b + 1)

            batches(act, batch)
            for g in range(4):
                for at in lag(B, g, 2, True) if g < 2 else ():
                    take_pT(*at)
                pick(B - 1, G - 4 + g)
                if g == 0:
                    take_xT(B - 2)
            take_xT(B - 1)

            def cast_weight(c, n, par):
                act.wait_ge(scaled, c * NPC + n + 1)
                slot = n % 2
                if n < 2 * SC:
                    if not isinstance(c, int) or c >= 2:
                        act.wait_ge(up_ready, (c - 1) * NT * SC)
                    dst = w_hi[:, par, n // 2, n % 2].rearrange("p k i -> p (k i)")
                else:
                    if not isinstance(c, int) or c >= 1:
                        act.wait_ge(down_ready, c * B)
                    dst = d_hi[:, n - 2 * SC, :]
                nc.scalar.activation(dst, raw_s[:, slot].rearrange("p k i -> p (k i)"), ACT.Copy)\
                    .then_inc(w_hi_ready, 1)

            def hidden(c, t, i):
                u = (c * NT + t) * SC + i
                act.wait_ge(gate_ready, u + 1)
                if not isinstance(c, int) or c > 0 or t > 0 or i > 0:
                    act.wait_ge(hid_ready, u)
                nc.scalar.activation(silu[:, :], gate_ps[i][:, :], ACT.Silu, scale=1.0 / (XS * WS))\
                    .then_inc(silu_ready, 1)
                act.wait_ge(hid_ready, u + 1)
                if not isinstance(c, int) or c > 0 or t > 1:
                    act.wait_ge(down_ready, (c * NT + t - 1) * TT)
                nc.scalar.activation(h_hi[:, t % 2, i, :], hid[:, :], ACT.Copy).then_inc(h_hi_ready, 1)

            for n in range(2 * SC):
                cast_weight(0, n, 0)

            def one(c, par, first, last):
                for t in range(NT):
                    for i in range(SC):
                        hidden(c, t, i)
                        if t == 0:
                            pass
                    if t == 0:
                        for i in range(SC):
                            cast_weight(c, 2 * SC + i, par)
                    if t in (1, 2) and not last:
                        for n in range(2 * (t - 1), 2 * t):
                            cast_weight(c + 1, n, 1 - par)

            passes(act, one)

        @block.vector
        def _(dve):
            dve.wait_ge(gates_ready, 1)

            def moments(b, src, which, s_stats, s_mv):
                for n in range(2):
                    nc.vector.bn_stats(out=stats[:, which, n, :], in_=src(n)).then_inc(s_stats, 1)
                both, = first_wait(dve, 2 * b + 2)
                dve.wait_ge(s_stats, both)
                nc.vector.bn_aggr(out=mv[:, which, :], in_=stats[:, which, :, :]).then_inc(s_mv, 1)

            def moments_x(b):
                loaded, before = first_wait(dve, 16 * (b + 1), b)
                dve.wait_ge(x_loaded, loaded)
                if not isinstance(b, int) or b > 0:
                    dve.wait_ge(x_normed, before)
                    dve.wait_ge(rstd_done, before)
                moments(b, lambda n: xt[:, n * HALF:(n + 1) * HALF], 0, stats_done, mv_done)

            def norm_x(b):
                dve.wait_ge(rstd_done, b + 1)
                if not isinstance(b, int) or b > 0:
                    dve.wait_ge(q_proj, 2 * b)
                if not isinstance(b, int) or b > 2:
                    dve.wait_ge(xT_ready, 2 * b - 4)
                nc.vector.tensor_scalar(xn[:, :], xt[:, :], mv[:, 0, 0:1], rstd[:, 0:1],
                                        ALU.subtract, ALU.mult).then_inc(x_normed, 1)

            def moments_row(b):
                whole, before = first_wait(dve, 2 * b + 2, b)
                dve.wait_ge(attended, whole)
                if not isinstance(b, int) or b > 0:
                    dve.wait_ge(row_normed, before)
                    dve.wait_ge(rstd2_done, before)
                moments(b, lambda n: rows[:, bass.ds(b, 1), n * HALF:(n + 1) * HALF].rearrange("p a t -> p (a t)"),
                        1, stats2_done, mv2_done)

            def norm_row(b, last):
                row = rows[:, bass.ds(b, 1), :].rearrange("p a t -> p (a t)")
                dve.wait_ge(rstd2_done, b + 1)
                dve.wait_ge(q_proj, 2 * B if last else 2 * b + 6)
                if not isinstance(b, int) or b > 0:
                    dve.wait_ge(xT_ready, 2 * b)
                nc.vector.tensor_scalar(xn[:, :], row, mv[:, 1, 0:1], rstd[:, 1:2],
                                        ALU.subtract, ALU.mult).then_inc(row_normed, 1)

            def soften(b, g, v_end=False):
                s = score[g % 2][:, 0:JQ * KW].rearrange("p (j k) -> p j k", k=KW)
                dve.wait_ge(scores_ready, G * b + g + 1)
                nc.vector.tensor_reduce(rmax[:, g % 2, :], s, AX.X, ALU.max).then_inc(max_ready, 1)
                if v_end:
                    take_v(b + 1, 0)
                dve.wait_ge(max_ready, G * b + g + 1)
                if not isinstance(b, int) or b > 0 or g >= 2:
                    dve.wait_ge(p_lo, G * b + g - 1)
                    dve.wait_ge(sum_ready, G * b + g - 1)
                nc.vector.tensor_tensor(pr[:, g % 2], s, rmax[:, g % 2, :].unsqueeze(2).to_broadcast([P, JQ, KW]),
                                        ALU.subtract).then_inc(shifted, 1)

            def total(b, g):
                dve.wait_ge(probs_ready, G * b + g + 1)
                if g == 0 and (not isinstance(b, int) or b > 0):
                    dve.wait_ge(rinv_ready, b)
                nc.vector.tensor_reduce(rsum[:, g % 2, g // 2 * JQ:(g // 2 + 1) * JQ], pr[:, g % 2],
                                        AX.X, ALU.add).then_inc(sum_ready, 1)

            def pick(b, g):
                q, hg = g // 2, g % 2
                dve.wait_ge(pv_ready, G * b + g + 1)
                if g == 0 and (not isinstance(b, int) or b > 0):
                    dve.wait_ge(oT_ready, b)
                src = mixed[g % 2].rearrange("p (j c) -> p j c", c=GC)
                for h in range(2, HG):
                    lo = QB * h
                    last = nc.vector.tensor_copy(on[lo:lo + QB, hg, q * JQ:(q + 1) * JQ, :],
                                                 src[lo:lo + QB, :, HD * h:HD * h + HD])
                last.then_inc(picked_dve, 1)

            def invert(b):
                dve.wait_ge(sum_ready, G * b + G)
                if not isinstance(b, int) or b > 0:
                    dve.wait_ge(o_scaled, b)
                nc.vector.reciprocal(rinv[:, :], rsum[:, :, :].rearrange("p g j -> p (g j)")).then_inc(rinv_ready, 1)

            def turn_o(b):
                dve.wait_ge(picked_act, G * (b + 1))
                dve.wait_ge(picked_dve, G * (b + 1))
                dve.wait_ge(rinv_ready, b + 1)
                o = on[:, :, :, :].rearrange("p g j d -> p (g j) d")
                nc.vector.tensor_tensor(o, o, rinv[:, :].unsqueeze(2).to_broadcast([P, 2 * NJ, HD]), ALU.mult)\
                    .then_inc(o_scaled, 1)
                dve.wait_ge(o_scaled, b + 1)
                if not isinstance(b, int) or b > 0:
                    dve.wait_ge(o_proj, 2 * b)
                nc.vector.transpose(oT[:, :, :].rearrange("p g n -> p (g n)"),
                                    on[:, :, :, :].rearrange("p g j d -> p (g j d)")).then_inc(oT_ready, 1)

            def add_attention(b):
                dve.wait_ge(residual_set, b + 1)
                for jj in range(2):
                    dve.wait_ge(o_proj, 2 * b + jj + 1)
                    row = rows[:, bass.ds(b, 1), :].rearrange("p a (j e t) -> p (a j) e t", e=2, t=QB)[:, :, jj, :]
                    nc.vector.scalar_tensor_tensor(
                        out=row, in0=proj[jj].rearrange("p (j t) -> p j t", t=QB), scalar=tanh_g[:, 0:1],
                        in1=row, op0=ALU.mult, op1=ALU.add).then_inc(attended, 1)

            def take_xT(b):
                for n in range(2):
                    dve.wait_ge(hi_ready, 2 * b + n + 1)
                    hi, lo = (xs[:, m, 4 * n:4 * n + 4, :].rearrange("p k r -> p (k r)") for m in range(2))
                    nc.vector.scalar_tensor_tensor(out=lo, in0=proj[n][:, :], scalar=XS, in1=hi,
                                                   op0=ALU.mult, op1=ALU.subtract).then_inc(lo_ready, 1)

            def take_v(b, n):
                dve.wait_ge(v_proj, 3 * b + n + 1)
                if n == 0 and (not isinstance(b, int) or b > 0):
                    dve.wait_ge(v_lo, b)
                if n == 0:
                    nc.vector.tensor_tensor(vn[0:WIN, 8, :], score[0][0:WIN, JQ * KW:HALF], bv_all[0:WIN, :],
                                            ALU.add).then_inc(v_nat, 1)
                else:
                    nc.vector.tensor_tensor(vn[:, 4 * n - 4:4 * n, :],
                                            proj[n - 1].rearrange("p (n c) -> p n c", c=C),
                                            bv_all[:, :].unsqueeze(1).to_broadcast([P, 4, C]), ALU.add)\
                        .then_inc(v_nat, 1)

            def spread_q(b, half):
                dve.wait_ge(q_moved, 64 * (b + 1))
                if not isinstance(b, int) or b > 0:
                    dve.wait_ge(scores_ready, G * (b - 1) + (half + 1) * (G // 2))
                n = NJ // 2
                for hg in range(2):
                    for h in range(HG):
                        last = nc.vector.tensor_scalar(
                            qm[:, hg, half * n:(half + 1) * n, h, :],
                            qs[:, hg, half * HALF:(half + 1) * HALF].rearrange("p (j t) -> p j t", t=QB),
                            head_of[:, h:h + 1], None, ALU.mult)
                last.then_inc(q_spread, 1)

            nc.vector.memset(vn[:, 8, :], 0.0).then_inc(vn_zeroed, 1)
            moments_x(0)
            norm_x(0)
            dve.wait_ge(consts_loaded, 16 * N_CONST)
            dve.wait_ge(vn_zeroed, 1)
            for n in range(3):
                take_v(0, n)
            dve.wait_ge(masks_made, 9)
            spread_q(0, 0)

            def batch(b, par, prev, next):
                for g in range(G):
                    soften(b, g, g == 2 and next)
                    for at in lag(b, g, 1, prev):
                        total(*at)
                    for at in lag(b, g, 4, prev):
                        pick(*at)
                    if g == 0 and next:
                        moments_x(b + 1)
                    if g == 1 and prev >= 2:
                        take_xT(b - 2)
                    if g == 1 and next:
                        norm_x(b + 1)
                    if g == 2:
                        spread_q(b, 1)
                    if g == 3 and prev:
                        turn_o(b - 1)
                    if g == 0 and prev:
                        invert(b - 1)
                    if g == 4 and next:
                        take_v(b + 1, 1)
                        take_v(b + 1, 2)
                    if g == 5 and prev:
                        add_attention(b - 1)
                        moments_row(b - 1)
                    if g == 6 and prev:
                        norm_row(b - 1, not next)
                    if g == 7 and next:
                        spread_q(b + 1, 0)

            batches(dve, batch)
            total(B - 1, G - 1)
            invert(B - 1)
            for g in range(4):
                pick(B - 1, G - 4 + g)
                if g == 1:
                    take_xT(B - 2)
            turn_o(B - 1)
            add_attention(B - 1)
            moments_row(B - 1)
            norm_row(B - 1, True)
            take_xT(B - 1)

            def scale_weight(c, n):
                slot = n % 2
                dve.wait_ge(zero_taken, c * NPC + n + 1)
                nc.vector.scalar_tensor_tensor(out=raw_s[:, slot].rearrange("p k i -> p (k i)"),
                                               in0=raw_z[:, slot].rearrange("p k i -> p (k i)"), scalar=WS,
                                               in1=raw_s[:, slot].rearrange("p k i -> p (k i)"),
                                               op0=ALU.mult, op1=ALU.mult).then_inc(scaled, 1)

            def hidden(c, t, i):
                u = (c * NT + t) * SC + i
                dve.wait_ge(up_ready, u + 1)
                dve.wait_ge(silu_ready, u + 1)
                if not isinstance(c, int) or c > 0 or t > 0 or i > 0:
                    dve.wait_ge(h_lo_ready, u)
                nc.vector.scalar_tensor_tensor(out=hid[:, :], in0=up_ps[i][:, :], scalar=1.0 / (XS * WS),
                                               in1=silu[:, :], op0=ALU.mult, op1=ALU.mult).then_inc(hid_ready, 1)
                dve.wait_ge(h_hi_ready, u + 1)
                nc.vector.tensor_tensor(h_lo[:, t % 2, i, :], hid[:, :], h_hi[:, t % 2, i, :], ALU.subtract)\
                    .then_inc(h_lo_ready, 1)

            def add_down(c, t):
                for r in range(TT):
                    n = (c * NT + t) * TT + r
                    dve.wait_ge(down_ready, n + 1)
                    if not isinstance(c, int) or c > 0:
                        dve.wait_ge(added, n - 2)
                    for half in range(2):
                        row = rows[:, t * TT + r, half * HALF:(half + 1) * HALF]
                        last = nc.vector.scalar_tensor_tensor(
                            out=row, in0=bank[4 + 2 * (r % 2) + half][:, :], scalar=ffn_gate[:, :], in1=row,
                            op0=ALU.mult, op1=ALU.add)
                    last.then_inc(added, 1)

            dve.wait_ge(scaled_bias, 2)
            for n in range(2 * SC):
                scale_weight(0, n)

            def one(c, par, first, last):
                for t in range(NT):
                    for i in range(SC):
                        hidden(c, t, i)
                    if t > 0:
                        add_down(c, t - 1)
                    elif not first:
                        add_down(c - 1, NT - 1)
                    if t == 0:
                        for i in range(SC):
                            scale_weight(c, 2 * SC + i)
                    if t in (1, 2) and not last:
                        for n in range(2 * (t - 1), 2 * t):
                            scale_weight(c + 1, n)

            passes(dve, one)
            add_down(NC - 1, NT - 1)

        @block.tensor
        def _(pe):
            pe.wait_ge(consts_loaded, 16 * N_CONST)
            pe.wait_ge(masks_made, 9)

            def bank_free(free):
                for s, count in free:
                    if not isinstance(count, int) or count > 0:
                        pe.wait_ge(s, count)

            def project_q(b, free):
                pe.wait_ge(x_normed, b + 1)
                for n in range(2):
                    bank_free(free(n))
                    nc.tensor.matmul(proj[n][:, :], wq[:, :], xn[:, n * HALF:(n + 1) * HALF],
                                     start=True, stop=True).then_inc(q_proj, 1)

            def project_k(b, free):
                pe.wait_ge(ctx_loaded, 16 * (b + 1))
                for n in range(2):
                    bank_free(free(n))
                    nc.tensor.matmul(proj[n][:, :], wk[:, :], ct[:, PAD + n * HALF:PAD + (n + 1) * HALF],
                                     start=True, stop=True).then_inc(k_proj, 1)

            def project_v(b, half, free):
                pe.wait_ge(ctx_loaded, 16 * (b + 1))
                bank_free(free)
                for j in range(4):
                    start = (4 * half + j) * P
                    last = nc.tensor.matmul(proj[half][:, j * C:(j + 1) * C], ct[:, start:start + P], wv[:, :],
                                            start=True, stop=True)
                last.then_inc(v_proj, 1)

            def project_v_end(b):
                pe.wait_ge(ctx_loaded, 16 * (b + 1))
                nc.tensor.matmul(score[0][0:QB, JQ * KW:HALF], ct[:, T:T + QB], wv[:, :], start=True, stop=True,
                                 skip_group_check=True).then_inc(v_proj, 1)

            def scores(b, g, par, v_end=False):
                q, hg = g // 2, g % 2
                if g == 0:
                    pe.wait_ge(k_moved, 64 * (b + 1))
                    pe.wait_ge(q_spread, 2 * b + 1)
                if g == G // 2:
                    pe.wait_ge(q_spread, 2 * b + 2)
                if not isinstance(b, int) or b > 0 or g >= 2:
                    pe.wait_ge(shifted, G * b + g - 1)
                if v_end:
                    project_v_end(b + 1)
                dst = score[g % 2][:, 0:JQ * KW].rearrange("p (j k) -> p j k", k=KW)
                nc.tensor.matmul(dst, spread[:, :, :].rearrange("p h t -> p (h t)"),
                                 window[:, :].unsqueeze(1).to_broadcast([P, JQ, KW]),
                                 start=True, stop=False, skip_group_check=True)
                for j in range(JQ):
                    t = QB * (JQ * q + j)
                    for part in range(2):
                        last = nc.tensor.matmul(dst[:, j, :], qm[:, hg, JQ * q + j, :, :].rearrange("p h t -> p (h t)"),
                                                ks[:, par, hg, part, t:t + KW], start=False,
                                                stop=(j == JQ - 1 and part == 1), skip_group_check=True)
                last.then_inc(scores_ready, 1)

            def turn_probs(b, g):
                pe.wait_ge(p_lo, G * b + g + 1)
                if not isinstance(b, int) or b > 0 or g >= 2:
                    pe.wait_ge(pT_ready, G * b + g - 1)
                for j in range(JQ):
                    last = nc.tensor.transpose(turned[g % 2][:, j * P:(j + 1) * P],
                                               p_hl[:, g % NP, j, :, :].rearrange("p h k -> p (h k)"), ident16[:, :])
                last.then_inc(probs_turned, 1)

            def mix(b, g, par):
                q, hg = g // 2, g % 2
                pe.wait_ge(pT_ready, G * b + g + 1)
                if g == 0:
                    pe.wait_ge(v_placed, 224 * (b + 1))
                if not isinstance(b, int) or b > 0 or g >= 2:
                    pe.wait_ge(picked_act, G * b + g - 1)
                    pe.wait_ge(picked_dve, G * b + g - 1)
                k = KP + KW
                for j in range(JQ):
                    for part in range(2):
                        last = nc.tensor.matmul(mixed[g % 2][:, j * GC:(j + 1) * GC],
                                                pT[0:k, g % 2, j * P:(j + 1) * P],
                                                vt[0:k, par, q * JQ + j, part, hg * GC:(hg + 1) * GC],
                                                start=(part == 0), stop=(part == 1))
                last.then_inc(pv_ready, 1)

            def project_o(b, free):
                pe.wait_ge(oT_ready, b + 1)
                for jj in range(2):
                    bank_free(free(jj))
                    for hg in range(2):
                        last = nc.tensor.matmul(proj[jj][:, :], wo[:, hg, jj, :], oT[:, hg, :],
                                                start=(hg == 0), stop=(hg == 1))
                    last.then_inc(o_proj, 1)

            def turn_x(b, free):
                pe.wait_ge(row_normed, b + 1)
                for n in range(2):
                    bank_free(free(n))
                    for k in range(4):
                        f = (4 * n + k) * P
                        last = nc.tensor.transpose(proj[n][:, k * P:(k + 1) * P], xn[:, f:f + P], ident[:, :])
                    last.then_inc(xT_ready, 1)

            project_k(0, lambda n: [])
            project_q(0, lambda n: [(k_nat, n + 1)])
            project_v_end(0)
            project_v(0, 0, [(q_nat, 1)])
            project_v(0, 1, [(q_nat, 2)])
            pe.wait_ge(v_nat, 3)

            def batch(b, par, prev, next):
                for g in range(G):
                    scores(b, g, par, g == 2 and next)
                    for at in lag(b, g, 2, prev):
                        turn_probs(*at)
                    for at in lag(b, g, 3, prev):
                        mix(*at, par if g >= 3 else 1 - par)
                    if g == 1 and next:
                        project_k(b + 1, lambda n: [(v_nat, 3 * b + 3)] + [(lo_ready, 2 * b - 2)] * bool(prev))
                    if g == 2 and next:
                        project_q(b + 1, lambda n: [(k_nat, 2 * b + n + 3)])
                    if g == 3 and next:
                        project_v(b + 1, 0, [(q_nat, 2 * b + 3)])
                        project_v(b + 1, 1, [(q_nat, 2 * b + 4)])
                    if g == 4 and prev:
                        project_o(b - 1, (lambda n: [(v_nat, 3 * b + 5 + n)]) if next else
                                  (lambda n: [(lo_ready, 2 * b - 2)]))
                    if g == 7 and prev:
                        turn_x(b - 1, lambda n: [(attended, 2 * b + n - 1)])

            batches(pe, batch)
            for g in range(3):
                for at in lag(B, g, 2, True) if g < 2 else ():
                    turn_probs(*at)
                mix(B - 1, G - 3 + g, 1)
            project_o(B - 1, lambda n: [(lo_ready, 2 * B - 2)])
            turn_x(B - 1, lambda n: [(attended, 2 * B)])

            pe.wait_ge(lo_ready, 2 * B)

            def gate_up(c, t, par):
                for i in range(SC):
                    u = (c * NT + t) * SC + i
                    for m, (ps, ready) in enumerate(((gate_ps, gate_ready), (up_ps, up_ready))):
                        if t == 0:
                            pe.wait_ge(w_lo_ready, c * NPC + 2 * i + m + 1)
                        if isinstance(c, int) and c == 0 and i == 0 and m == 0:
                            pe.wait_ge(xT_loaded[t], 16 * TT)
                        if not isinstance(c, int) or c > 0 or t > 0:
                            pe.wait_ge((silu_ready, hid_ready)[m], u - 1)
                        for k in range(NK):
                            hi, lo = w_hi[:, par, i, m, k, :], w_lo[:, par, i, m, k, :]
                            xh, xl = xT[:, t * TT:(t + 1) * TT, 0, k, :], xT[:, t * TT:(t + 1) * TT, 1, k, :]
                            nc.tensor.matmul(ps[i][:, :], hi, xh, start=(k == 0), stop=False)
                            nc.tensor.matmul(ps[i][:, :], hi, xl, start=False, stop=False)
                            last = nc.tensor.matmul(ps[i][:, :], lo, xh, start=False, stop=(k == NK - 1))
                        last.then_inc(ready, 1)

            def down(c, t, par):
                pe.wait_ge(h_lo_ready, (c * NT + t + 1) * SC)
                if t == 0:
                    pe.wait_ge(w_lo_ready, (c + 1) * NPC)
                for r in range(TT):
                    n = (c * NT + t) * TT + r
                    if not isinstance(c, int) or c > 0 or t > 0 or r > 1:
                        pe.wait_ge(added, n - 1)
                    for half in range(2):
                        ps = bank[4 + 2 * (r % 2) + half]
                        for i in range(SC):
                            hh, hl = h_hi[:, t % 2, i, r * P:(r + 1) * P], h_lo[:, t % 2, i, r * P:(r + 1) * P]
                            dh = d_hi[:, i, half * HALF:(half + 1) * HALF]
                            dl = d_lo[:, i, half * HALF:(half + 1) * HALF]
                            nc.tensor.matmul(ps[:, :], hh, dh, start=(i == 0), stop=False)
                            nc.tensor.matmul(ps[:, :], hh, dl, start=False, stop=False)
                            last = nc.tensor.matmul(ps[:, :], hl, dh, start=False, stop=(i == SC - 1))
                    last.then_inc(down_ready, 1)

            def one(c, par, first, last):
                for t in range(NT):
                    gate_up(c, t, par)
                    if t > 0:
                        down(c, t - 1, par)
                    elif not first:
                        down(c - 1, NT - 1, par)

            passes(pe, one)
            down(NC - 1, NT - 1, 1)


_INS = ['x', 'ctx_4096', 'g_xattn', 'g_ffn', 'L0_xattn_Wq', 'L0_xattn_bq', 'L0_xattn_Wk', 'L0_xattn_bk',
        'L0_xattn_Wv', 'L0_xattn_bv', 'L0_xattn_Wo', 'L0_xattn_bo', 'L0_ffn_gate_w', 'L0_ffn_gate_z',
        'L0_ffn_gate_s', 'L0_ffn_up_w', 'L0_ffn_up_z', 'L0_ffn_up_s', 'L0_ffn_down_w', 'L0_ffn_down_z',
        'L0_ffn_down_s']
_TRANSPOSED = ('L0_xattn_Wq', 'L0_xattn_Wk', 'L0_xattn_Wv', 'L0_xattn_Wo')


def kernel(**inputs):
    import numpy as _np
    import concourse.bacc as _bacc
    from concourse import mybir as _mybir
    from concourse.bass_utils import run_bass_kernel_spmd as _run

    nc = _bacc.Bacc("TRN2", target_bir_lowering=False, num_devices=1)
    arrays, args = {}, []
    for name in _INS:
        a = _np.asarray(inputs[name])
        a = _np.ascontiguousarray(a.T if name in _TRANSPOSED else a)
        arrays[f"in_{name}_dram"] = a
        args.append(nc.dram_tensor(f"in_{name}_dram", a.shape, _mybir.dt.from_np(a.dtype), kind="ExternalInput").ap())
    args.append(nc.dram_tensor("out_0_dram", (16, 128, 1024), _mybir.dt.float32, kind="ExternalOutput").ap())
    flamingo_layer(nc, *args)
    r = _run(nc, [arrays], core_ids=[0])
    return r.results[0]["out_0_dram"]
```

```python
import concourse.bass as bass
from concourse import mybir
from contextlib import ExitStack


def flamingo_layer(nc, x_in, ctx_in, g_xattn, g_ffn, WqT, bq, WkT, bk, WvT, bv, WoT, bo,
                   gate_w, gate_z, gate_s, up_w, up_z, up_s, down_w, down_z, down_s, out):
    fp32, fp16, bf16, i32 = mybir.dt.float32, mybir.dt.float16, mybir.dt.bfloat16, mybir.dt.int32
    ALU, ACT, AX = mybir.AluOpType, mybir.ActivationFunctionType, mybir.AxisListType
    P = 128

    B, C, T = x_in.shape
    HEADS, WIN = 8, 16
    HD = C // HEADS
    PAD = WIN // 2
    QB = 32
    KW = QB + WIN
    KP = 64
    NJ = T // QB
    HG = 4
    GC = HG * HD
    NQ = 4
    JQ = NJ // NQ
    G = NQ * 2
    HALF = 512
    EPS = 1e-5
    MASKED = -1e30

    F = gate_w.shape[1]
    NK = T // P
    SC = 2
    NC = F // (P * SC)
    ROWS = B * C
    TB = 1024
    NT = ROWS // TB
    TT = TB // P
    NQT = NT * SC
    QU = 3 * NK
    NU = NQT * QU
    QG = 2 * NK
    QS = QG - 2
    NCT = T // P
    LAG = NK + 3
    D_DVE = (2, 7)
    XS = 256.0
    KH = NK // 2
    NGU = 4 * SC
    ND = 2 * SC
    NPC = NGU + ND

    ctx = ExitStack()
    with ctx:
        def sb(name, shape, dt, stack=ctx):
            return stack.enter_context(nc.sbuf_tensor(name, shape, dt))

        def sem(name):
            return ctx.enter_context(nc.semaphore(name))

        xT = sb("xT", [P, B, 2, NK, P], fp16)
        ident = sb("ident", [P, P], fp32)
        gates = sb("gates", [P, 2], fp32)
        tanh_g = sb("tanh_g", [P, 2], fp32)
        scales = sb("scales", [P, F // P, 3, NK], fp32)
        scale = sb("scale", [P, 2, SC, 3, NK], fp32)
        def as_rows(b, n=1):
            return xT[:, b:b + n].rearrange("p b h k r -> p (b h k r)").bitcast(fp32)

        gu_stage, d_stage = as_rows(B - 4, 4), as_rows(B - 5)

        att = ExitStack()
        CW = PAD + T + 24
        xt = sb("xt", [P, T], fp32, att)
        ct = sb("ct", [P, CW], fp32, att)
        nat = sb("nat", [P, T], fp32, att)
        k_hl = sb("k_hl", [P, 2, T], fp16, att)
        q_hl = sb("q_hl", [P, 2, T], fp16, att)
        vn = sb("vn", [P, 9, C], fp32, att)
        vn_hl = sb("vn_hl", [P, 9, 2, C], fp16, att)
        wq = sb("wq", [P, C], fp32, att)
        wk = sb("wk", [P, C], fp32, att)
        wv = sb("wv", [P, C], fp32, att)
        bias = sb("bias", [P, 3], fp32, att)
        bv_all = sb("bv_all", [P, C], fp32, att)
        head_of = sb("head_of", [P, HG], fp32, att)
        ident16 = sb("ident16", [P, P], fp16, att)
        spread = sb("spread", [P, HG, QB], bf16, att)
        window = sb("window", [P, KW], bf16, att)
        qs = sb("qs", [P, 2, T], fp16, att)
        qm = sb("qm", [P, 2, NJ, HG, QB], fp16, att)
        ks = sb("ks", [P, 2, 2, 2, T + WIN], fp16, att)
        vt = sb("vt", [P, 2, NJ, 2, C], fp16, att)
        NP = 2
        p_hl = sb("p_hl", [P, NP, JQ, 2, KP], fp16, att)
        pT = sb("pT", [P, 2, JQ * P], fp16, att)
        wo = sb("wo", [P, 2, 2, C], fp32, att)
        bo_g = sb("bo_g", [P, 1], fp32, att)
        xn = sb("xn", [P, T], fp32, att)
        stats = sb("stats", [P, 2, 2, 6], fp32, att)
        mv = sb("mv", [P, 2, 2], fp32, att)
        var_eps = sb("var_eps", [P, 2], fp32, att)
        minus_half = sb("minus_half", [P, 1], fp32, att)
        rstd = sb("rstd", [P, 2], fp32, att)
        pr = sb("pr", [P, 2, JQ, KW], fp32, att)
        rmax = sb("rmax", [P, 2, JQ], fp32, att)
        rsum = sb("rsum", [P, 2, NJ], fp32, att)
        rinv = sb("rinv", [P, 2 * NJ], fp32, att)
        on = sb("on", [P, 2, NJ, HD], fp32, att)
        oT = sb("oT", [P, 2, HALF], fp32, att)
        rows = sb("rows", [P, 2, T], fp32, att)
        att.close()

        raw_w = sb("raw_w", [P, 2, KH, P], i32)
        raw_z = sb("raw_z", [P, 2, KH, P], i32)
        w_int = sb("w_int", [P, 2, SC, 2, NK, P], fp16)
        d_int = sb("d_int", [P, 2, SC, T], fp16)
        acc = sb("acc", [P, 2, 2, TB], fp32)
        h_hi = sb("h_hi", [P, 2, TB], fp16)
        h_lo = sb("h_lo", [P, 2, TB], fp16)
        d_part = sb("d_part", [P, 2, TB], fp32)
        oacc = sb("oacc", [P, NCT, NT, TB], fp32)
        row_dram = nc.dram_tensor("rows_after_attention", (B, P, T), fp32, kind="Internal").ap()

        pair = [ctx.enter_context(nc.psum_tensor(f"bank{n}", [P, 2, HALF], fp32)) for n in range(4)]
        bank = [pair[n // 2][:, n % 2, :] for n in range(8)]
        proj = bank[0:2]
        score = bank[2:4]
        turned = [ctx_t[:, :].bitcast(fp16) for ctx_t in bank[4:6]]
        mixed = bank[6:8]

        consts_loaded, gates_loaded, wo_loaded = sem("consts_loaded"), sem("gates_loaded"), sem("wo_loaded")
        vt_zeroed = sem("vt_zeroed")
        zeroed, consts_made, masks_made, gates_ready, scaled_bias = (
            sem("zeroed"), sem("consts_made"), sem("masks_made"), sem("gates_ready"), sem("scaled_bias"))
        x_loaded, ctx_loaded, q_moved, k_moved, v_placed, q_spread = (
            sem("x_loaded"), sem("ctx_loaded"), sem("q_moved"), sem("k_moved"), sem("v_placed"), sem("q_spread"))
        row_loaded, residual_set, row_kept = sem("row_loaded"), sem("residual_set"), sem("row_kept")
        eps_added = [sem("eps_added"), sem("eps2_added")]
        stats_done, mv_done, rstd_done, x_normed = sem("stats_done"), sem("mv_done"), sem("rstd_done"), sem("x_normed")
        q_proj, k_proj, v_proj, o_proj, xT_ready = (
            sem("q_proj"), sem("k_proj"), sem("v_proj"), sem("o_proj"), sem("xT_ready"))
        q_nat, k_nat, v_nat = sem("q_nat"), sem("k_nat"), sem("v_nat")
        q_hi, k_hi, v_hi, p_hi = sem("q_hi"), sem("k_hi"), sem("v_hi"), sem("p_hi")
        q_lo, k_lo, v_lo, p_lo = sem("q_lo"), sem("k_lo"), sem("v_lo"), sem("p_lo")
        scores_ready, max_ready, shifted, probs_ready, sum_ready, folded = (
            sem("scores_ready"), sem("max_ready"), sem("shifted"), sem("probs_ready"), sem("sum_ready"),
            sem("folded"))
        probs_turned, pT_ready, pv_ready = sem("probs_turned"), sem("pT_ready"), sem("pv_ready")
        picked = sem("picked")
        rinv_ready, o_scaled, oT_ready, attended = (
            sem("rinv_ready"), sem("o_scaled"), sem("oT_ready"), sem("attended"))
        stats2_done, mv2_done, rstd2_done, row_normed = (
            sem("stats2_done"), sem("mv2_done"), sem("rstd2_done"), sem("row_normed"))
        hi_ready, lo_ready, vn_zeroed = sem("hi_ready"), sem("lo_ready"), sem("vn_zeroed")
        s_loaded, s_turned, s_kept = sem("s_loaded"), sem("s_turned"), sem("s_kept")

        raw_loaded = [sem("raw0_loaded"), sem("raw1_loaded")]
        zero_taken, w_cast, scale_ready = sem("zero_taken"), sem("w_cast"), sem("scale_ready")
        unit_ready, acc_started, summed, silu_ready, hid_ready, h_hi_ready, h_lo_ready = (
            sem("unit_ready"), sem("acc_started"), sem("summed"), sem("silu_ready"), sem("hid_ready"),
            sem("h_hi_ready"), sem("h_lo_ready"))
        down_ready, d_summed, d_scaled, d_added = (
            sem("down_ready"), sem("d_summed"), sem("d_scaled"), sem("d_added"))
        row_back = [sem(f"rows_of_block{t}_back") for t in range(NT)]
        out_turned, out_ready = sem("out_turned"), sem("out_ready")
        stored, oacc_zeroed = sem("stored"), sem("oacc_zeroed")

        N_CONST = 7

        def batches(eng, batch):
            batch(0, 0, 0, 2)
            batch(1, 1, 1, 2)
            with eng.Fori(1, B // 2 - 1) as i:
                batch(2 * i, 0, 2, 2)
                batch(2 * i + 1, 1, 2, 2)
            batch(B - 2, 0, 2, 1)
            batch(B - 1, 1, 2, 0)

        ZERO_AT, CAST_AT = (1, 2, 4, 5, 7), (2, 3, 5, 6)

        LAST_O, LAST_ADD, LAST_STD, LAST_NORM, LAST_TURN, LAST_XT = 8, 9, 10, 15, 20, 21
        ZERO_SUMS_AT, EARLY_TILES = (1, 4, 7, 12, 25, 29, 31, 34), 4

        def lag(b, g, n, prev):
            if g >= n:
                return [(b, g - n)]
            return [(b - 1, G + g - n)] if prev else []

        def quarter(u):
            q = u // QU
            return q, q // SC, q % SC, u % QU // 3, u % 3

        def down_unit(c, u):
            x = u // 3 - LAG
            return None if isinstance(c, int) and NQT * NK * c + x < 0 else x

        def count(c, x, mine):
            own = [r for r in range(NK) if ((r + LAG) % NK in D_DVE) == mine]
            return c * NQT * len(own) + x // NK * len(own) + sum(r <= x % NK for r in own)

        def by_dve(x):
            return (x + LAG) % NK in D_DVE

        def down_emptied(c, x):
            return (d_summed if by_dve(x) else d_scaled), count(c, x, by_dve(x))

        def emptied(c, u):
            before = u - 4
            while True:
                cc, v = (c - 1, before + NU) if before < 0 else (c, before)
                if isinstance(cc, int) and cc < 0:
                    return None
                q, t, i, k, m = quarter(v)
                if m < 2 and k == 0:
                    return acc_started, (cc * NQT + q) * 2 + m + 1
                if m < 2:
                    return summed, (cc * NQT + q) * QS + 2 * k + m - 1
                if down_unit(cc, v) is not None:
                    return down_emptied(cc, down_unit(cc, v))
                before -= 4

        def due(c, u, late, last):
            j, at = (u - late) // 8, (u - late) % 8
            if u < late or at or j >= NPC:
                return []
            if j < ND:
                return [(c, NGU + j)]
            return [] if last else [(c + 1, j - ND)]

        left = [("down", x) for x in range(NQT * NK - LAG, NQT * NK)]
        end = []
        for n in range(max(len(left), TT)):
            end += left[n:n + 1] + ([("out", n)] if n < TT else [])
        end += [("out", b) for b in range(TT, B)]

        def end_emptied(n):
            if n < 4:
                return emptied(NC - 1, NU + n)
            kind, x = end[n - 4]
            return (out_ready, x + 1) if kind == "out" else down_emptied(NC - 1, x)

        def passes(eng, one):
            one(0, 0, True, False)
            with eng.Fori(0, (NC - 2) // 2) as i:
                one(2 * i + 1, 1, False, False)
                one(2 * i + 2, 0, False, False)
            one(NC - 1, 1, False, True)

        def first_wait(eng, *values):
            values = [v if isinstance(v, int) else eng.snap(eng.to_reg(v)) for v in values]
            eng.wait_ge(consts_made, 5)
            return values

        block = ctx.enter_context(nc.Block())

        @block.sync
        def _(sp):
            sp.dma_start(xt[:, :], x_in[0]).then_inc(x_loaded, 16)
            sp.dma_start(ct[:, PAD:PAD + T], ctx_in[0]).then_inc(ctx_loaded, 16)
            sp.dma_start(wk[:, :], WkT).then_inc(consts_loaded, 16)
            sp.dma_start(wq[:, :], WqT).then_inc(consts_loaded, 16)
            for n, v in enumerate((bq, bk, bo)):
                sp.dma_start(bias[:, n:n + 1], v.rearrange("(p a) -> p a", a=1)).then_inc(consts_loaded, 16)
            sp.dma_start(wv[:, :], WvT).then_inc(consts_loaded, 16)
            sp.dma_start(bv_all[:, :], bv.partition_broadcast(P)).then_inc(consts_loaded, 16)
            for n, v in enumerate((g_xattn, g_ffn)):
                sp.dma_start(gates[:, n:n + 1], v.partition_broadcast(P)).then_inc(gates_loaded, 16)
            for m, v in enumerate((gate_s, up_s)):
                sp.dma_start(gu_stage[m * NK:(m + 1) * NK, 0:F], v).then_inc(s_loaded, 16)
            sp.dma_start(d_stage[0:F // P, :], down_s).then_inc(s_loaded, 16)

            def load_x(b):
                used, = first_wait(sp, b)
                if not isinstance(b, int) or b > 0:
                    sp.wait_ge(x_normed, used)
                sp.dma_start(xt[:, :], x_in[bass.ds(b, 1)].rearrange("a c t -> (a c) t")).then_inc(x_loaded, 16)

            def load_ctx(b):
                used, = first_wait(sp, 3 * b)
                sp.wait_ge(v_proj, used)
                sp.dma_start(ct[:, PAD:PAD + T], ctx_in[bass.ds(b, 1)].rearrange("a c t -> (a c) t"))\
                  .then_inc(ctx_loaded, 16)

            def move_k(b, par):
                ready, used = first_wait(sp, b + 1, G * (b - 1))
                sp.wait_ge(k_lo, ready)
                if not isinstance(b, int) or b > 1:
                    sp.wait_ge(scores_ready, used)
                for hg in range(2):
                    for copy in range(2):
                        sp.dma_start(ks[GC * copy:GC * copy + GC, par, hg, :, PAD:PAD + T],
                                     k_hl[GC * hg:GC * hg + GC, :, :]).then_inc(k_moved, 16)

            def move_q(b):
                ready, used = first_wait(sp, b + 1, 2 * b)
                sp.wait_ge(q_lo, ready)
                if not isinstance(b, int) or b > 0:
                    sp.wait_ge(q_spread, used)
                for hg in range(2):
                    for part in range(2):
                        sp.dma_start(qs[GC * part:GC * part + GC, hg, :],
                                     q_hl[GC * hg:GC * hg + GC, part, :]).then_inc(q_moved, 16)

            def place_v(b, par):
                ready, used = first_wait(sp, b + 1, G * (b - 1))
                sp.wait_ge(v_lo, ready)
                if not isinstance(b, int) or b > 1:
                    sp.wait_ge(pv_ready, used)
                for d in (0, KP):
                    for dst, src in (
                            (vt[d + PAD:d + KW, par, 0], vn_hl[PAD:KW, 0]),
                            (vt[d:d + KW, par, 4:NJ:4], vn_hl[0:KW, 1:8]),
                            (vt[d:d + KW, par, 1:NJ:4], vn_hl[QB:QB + KW, 0:8]),
                            (vt[d:d + KW, par, 2:NJ:4], vn_hl[2 * QB:2 * QB + KW, 0:8]),
                            (vt[d:d + QB, par, 3:NJ:4], vn_hl[3 * QB:P, 0:8]),
                            (vt[d + QB:d + KW, par, 3:NJ - 1:4], vn_hl[0:WIN, 1:8]),
                            (vt[d + QB:d + QB + PAD, par, NJ - 1], vn_hl[0:PAD, 8])):
                        sp.dma_start(dst, src).then_inc(v_placed, 16)

            def load_wo():
                for h in range(HG):
                    for hg in range(2):
                        for jj in range(2):
                            lo = QB * h + HD * jj
                            src = HD * (HG * hg + h)
                            sp.dma_start(wo[lo:lo + HD, hg, jj, :], WoT[src:src + HD, :]).then_inc(wo_loaded, 16)

            def load_row(b, par):
                kept, used = first_wait(sp, 16 * (b - 1), b - 1)
                if not isinstance(b, int) or b > 1:
                    sp.wait_ge(row_kept, kept)
                    sp.wait_ge(row_normed, used)
                sp.dma_start(rows[:, par, :], x_in[bass.ds(b, 1)].rearrange("a c t -> (a c) t"))\
                  .then_inc(row_loaded, 16)

            def keep_row(b, par):
                done, = first_wait(sp, 2 * b + 2)
                sp.wait_ge(attended, done)
                sp.dma_start(row_dram[bass.ds(b, 1)].rearrange("a p n -> (a p) n"), rows[:, par, :])\
                  .then_inc(row_kept, 16)

            def load_piece(c, n, first=False):
                slot = n % 2
                used, = first_wait(sp, c * NPC + n - 1)
                if not first:
                    sp.wait_ge(w_cast, used)
                if n < NGU:
                    ww, zz = ((gate_w, gate_z), (up_w, up_z))[n % 2]
                    col, k = (c * SC + n // 4) * P, n // 2 % 2 * KH
                    src = ww[k * P:(k + KH) * P, bass.ds(col, P)].rearrange("(k p) i -> p k i", p=P)
                    zrc = zz[k:k + KH, bass.ds(col, P)].partition_broadcast(P)
                else:
                    r, col = c * SC + (n - NGU) // 2, n % 2 * KH * P
                    src = down_w[bass.ds(r * P, P), col:col + KH * P].rearrange("p (k i) -> p k i", k=KH)
                    zrc = down_z[bass.ds(r, 1), col:col + KH * P].rearrange("a (k i) -> (a k) i", k=KH)\
                        .partition_broadcast(P)
                sp.dma_start(raw_w[:, slot], src).then_inc(raw_loaded[slot], 16)
                sp.dma_start(raw_z[:, slot], zrc).then_inc(raw_loaded[slot], 16)

            def first_weights(pieces):
                for n in pieces:
                    if n == 0:
                        sp.wait_ge(x_normed, B)
                        sp.wait_ge(v_proj, 3 * B)
                        sp.wait_ge(k_moved, 64 * B)
                        sp.wait_ge(q_moved, 64 * B)
                        sp.wait_ge(v_lo, B)
                    load_piece(0, n, n < 2)

            load_x(1)
            sp.wait_ge(zeroed, 5)
            move_k(0, 0)
            move_q(0)
            load_ctx(1)
            sp.wait_ge(vt_zeroed, 1)
            place_v(0, 0)
            sp.wait_ge(zeroed, 7)

            def batch(b, par, prev, next):
                load_row(b, par)
                if isinstance(b, int) and b == 1:
                    load_wo()
                if not next:
                    first_weights(range(4))
                if next >= 2:
                    load_x(b + 2)
                if next:
                    move_k(b + 1, 1 - par)
                if next >= 2:
                    load_ctx(b + 2)
                if next:
                    move_q(b + 1)
                if prev:
                    keep_row(b - 1, 1 - par)
                if next:
                    place_v(b + 1, 1 - par)

            batches(sp, batch)
            first_weights(range(4, NGU))


            def one(c, par, first, last):
                for n in range(NGU, NPC):
                    load_piece(c, n)
                    if first and n == NGU + 1:
                        keep_row(B - 1, 1)
                if not last:
                    for n in range(NGU):
                        load_piece(c + 1, n)

            passes(sp, one)

            for b in range(B):
                if b % TT == 0:
                    sp.wait_ge(unit_ready, (NC * NQT - (NT - 1 - b // TT) * SC) * QG)
                sp.dma_start(as_rows(b), row_dram[b]).then_inc(row_back[b // TT], 16)
            for b in range(B):
                sp.wait_ge(out_ready, b + 1)
                sp.dma_start(out[b], as_rows(b)).then_inc(stored, 16)
            sp.wait_ge(stored, 16 * B)

        @block.gpsimd
        def _(pool):
            nc.gpsimd.memset(ct[:, 0:PAD], 0.0).then_inc(zeroed, 1)
            nc.gpsimd.memset(ct[:, PAD + T:CW], 0.0).then_inc(zeroed, 1)
            nc.gpsimd.memset(wo[:, :, :, :], 0.0).then_inc(zeroed, 1)
            nc.gpsimd.memset(ks[:, :, :, :, 0:PAD].rearrange("p a g h k -> p (a g h) k"), 0.0).then_inc(zeroed, 1)
            nc.gpsimd.memset(ks[:, :, :, :, PAD + T:T + WIN].rearrange("p a g h k -> p (a g h) k"), 0.0)\
                .then_inc(zeroed, 1)
            nc.gpsimd.memset(p_hl[:, :, :, :, KW:KP].rearrange("p n j h k -> p (n j h) k"), 0.0).then_inc(zeroed, 1)
            nc.gpsimd.memset(head_of[:, :], 1.0).then_inc(consts_made, 1)
            nc.gpsimd.memset(minus_half[:, :], -0.5).then_inc(consts_made, 1)
            nc.gpsimd.memset(ident[:, :], 0.0).then_inc(consts_made, 1)
            nc.gpsimd.memset(spread[:, :, :], 0.0).then_inc(consts_made, 1)
            nc.gpsimd.memset(window[:, :], 0.0).then_inc(consts_made, 1)
            pool.wait_ge(consts_made, 5)
            nc.gpsimd.affine_select(out=ident[:, :], in_=ident[:, :], compare_op=ALU.not_equal, fill=1.0,
                                    base=0, pattern=[[-1, P]], channel_multiplier=1).then_inc(masks_made, 1)
            sp_rows, win = spread[0:QB, :, :], window[0:QB, :]
            nc.gpsimd.affine_select(out=sp_rows, in_=sp_rows, compare_op=ALU.not_equal, fill=1.0, base=0,
                                    pattern=[[0, HG], [-1, QB]], channel_multiplier=1).then_inc(masks_made, 1)
            nc.gpsimd.affine_select(out=win, in_=win, compare_op=ALU.is_ge, fill=MASKED, base=0,
                                    pattern=[[1, KW]], channel_multiplier=-1).then_inc(masks_made, 1)
            pool.wait_ge(masks_made, 3)
            nc.gpsimd.affine_select(out=win, in_=win, compare_op=ALU.is_ge, fill=MASKED, base=WIN - 1,
                                    pattern=[[-1, KW]], channel_multiplier=1).then_inc(masks_made, 1)
            nc.gpsimd.tensor_copy(ident16[:, :], ident[:, :]).then_inc(masks_made, 1)
            for n, lo in enumerate((0, GC)):
                mine = head_of[lo:lo + GC, :]
                nc.gpsimd.affine_select(out=mine, in_=mine, compare_op=ALU.is_ge, fill=0.0, base=0,
                                        pattern=[[-HD, HG]], channel_multiplier=1).then_inc(masks_made, 1)
                pool.wait_ge(masks_made, 6 + 2 * n)
                nc.gpsimd.affine_select(out=mine, in_=mine, compare_op=ALU.is_ge, fill=0.0, base=HD - 1,
                                        pattern=[[HD, HG]], channel_multiplier=-1).then_inc(masks_made, 1)

            pool.wait_ge(masks_made, 9)

            def inverse_std(b, which, moments_ready, used, done):
                now, before = first_wait(pool, b + 1, b)
                pool.wait_ge(moments_ready, now)
                if not isinstance(b, int) or b > 0:
                    pool.wait_ge(used, before)
                nc.gpsimd.tensor_scalar(var_eps[:, which:which + 1], mv[:, which, 1:2], EPS, None, ALU.add)\
                    .then_inc(eps_added[which], 1)
                pool.wait_ge(eps_added[which], b + 1)
                nc.gpsimd.tensor_tensor(rstd[:, which:which + 1], var_eps[:, which:which + 1], minus_half[:, :],
                                        ALU.pow)\
                    .then_inc(done, 1)

            def low_k(b):
                pool.wait_ge(k_hi, b + 1)
                nc.gpsimd.tensor_tensor(k_hl[:, 1, :], nat[:, :], k_hl[:, 0, :], ALU.subtract).then_inc(k_lo, 1)

            def low_q(b):
                pool.wait_ge(q_hi, b + 1)
                nc.gpsimd.tensor_tensor(q_hl[:, 1, :], xn[:, :], q_hl[:, 0, :], ALU.subtract).then_inc(q_lo, 1)

            def low_v(b):
                pool.wait_ge(v_hi, b + 1)
                nc.gpsimd.tensor_tensor(vn_hl[:, :, 1, :], vn[:, :, :], vn_hl[:, :, 0, :], ALU.subtract)\
                    .then_inc(v_lo, 1)

            def low_p(b, g):
                n, = first_wait(pool, G * b + g + 1)
                pool.wait_ge(p_hi, n)
                nc.gpsimd.tensor_tensor(p_hl[:, g % NP, :, 1, 0:KW], pr[:, g % 2], p_hl[:, g % NP, :, 0, 0:KW],
                                        ALU.subtract).then_inc(p_lo, 1)

            def fold(b, g):
                for n, half in enumerate((KW // 2, KW // 4)):
                    done, = first_wait(pool, 2 * (G * b + g) + n)
                    if n == 0:
                        pool.wait_ge(p_lo, G * b + g + 1)
                    else:
                        pool.wait_ge(folded, done)
                    a = pr[:, g % 2, :, 0:half]
                    nc.gpsimd.tensor_tensor(a, a, pr[:, g % 2, :, half:2 * half], ALU.add).then_inc(folded, 1)

            def take_zero(c, n):
                slot = n % 2
                pool.wait_ge(raw_loaded[slot], (c * (NPC // 2) + n // 2 + 1) * 32)
                nc.gpsimd.tensor_tensor(raw_z[:, slot], raw_w[:, slot], raw_z[:, slot], ALU.subtract)\
                    .then_inc(zero_taken, 1)

            inverse_std(0, 0, mv_done, x_normed, rstd_done)
            nc.gpsimd.memset(vt[:, 1].rearrange("p j h c -> p (j h c)").bitcast(fp32), 0.0).then_inc(zeroed, 1)
            low_k(0)
            low_q(0)
            low_v(0)

            def batch(b, par, prev, next):
                for g in range(G):
                    low_p(b, g)
                    if g == 0 and next:
                        inverse_std(b + 1, 0, mv_done, x_normed, rstd_done)
                    fold(b, g)
                    if g == 2 and next:
                        low_k(b + 1)
                    if g == 3 and next:
                        low_q(b + 1)
                    if g == 5 and prev:
                        inverse_std(b - 1, 1, mv2_done, row_normed, rstd2_done)
                    if g == 6 and next:
                        low_v(b + 1)
                    if not next and g in ZERO_AT:
                        take_zero(0, ZERO_AT.index(g))

            batches(pool, batch)

            def low_hidden(c, q):
                c, q = (c - 1, NQT - 1) if q < 0 else (c, q)
                pool.wait_ge(h_hi_ready, c * NQT + q + 1)
                nc.gpsimd.tensor_tensor(h_lo[:, q % 2, :], acc[:, q % 2, 0, :], h_hi[:, q % 2, :], ALU.subtract)\
                    .then_inc(h_lo_ready, 1)

            def add_down(c, x):
                n = count(c, x, False)
                pool.wait_ge(d_scaled, n)
                if not isinstance(n, int) or n > 1:
                    pool.wait_ge(d_added, n - 1)
                else:
                    pool.wait_ge(oacc_zeroed, NCT)
                part = d_part[:, (count(0, x, False) - 1) % 2, :]
                into = oacc[:, x % NCT, x // NCT // SC % NT, :]
                nc.gpsimd.tensor_tensor(into, into, part, ALU.add).then_inc(d_added, 1)

            for n in range(len(ZERO_AT), NGU):
                take_zero(0, n)
            def zero_sums(tile):
                if tile == 0:
                    pool.wait_ge(unit_ready, 1)
                if tile == EARLY_TILES:
                    pool.wait_ge(row_kept, 16 * B)
                    pool.wait_ge(lo_ready, 2 * B)
                nc.gpsimd.memset(oacc[:, tile], 0.0).then_inc(oacc_zeroed, 1)

            def one(c, par, first, last):
                for u in range(NU):
                    for at in due(c, u, 0, last):
                        take_zero(*at)
                    if first and u in ZERO_SUMS_AT:
                        zero_sums(ZERO_SUMS_AT.index(u))
                    if first and u == LAST_STD:
                        inverse_std(B - 1, 1, mv2_done, row_normed, rstd2_done)
                    if u % QU == 4 and not (first and u == 4):
                        low_hidden(c, u // QU - 1)
                    x = down_unit(c, u)
                    if u % 3 == 2 and x is not None and not by_dve(x):
                        add_down(c, x)

            passes(pool, one)
            low_hidden(NC, -1)
            for kind, x in end:
                if kind == "down" and not by_dve(x):
                    add_down(NC - 1, x)

        @block.scalar
        def _(act):
            act.wait_ge(gates_loaded, 32)
            nc.scalar.activation(tanh_g[:, :], gates[:, :], ACT.Tanh).then_inc(gates_ready, 1)
            act.wait_ge(gates_ready, 1)
            act.wait_ge(consts_loaded, 16 * N_CONST)
            nc.scalar.activation(bo_g[:, :], bias[:, 2:3], ACT.Identity, scale=tanh_g[:, 0:1]).then_inc(scaled_bias, 1)
            act.wait_ge(scaled_bias, 1)
            act.wait_ge(zeroed, 6)

            def set_residual(b, par):
                act.wait_ge(row_loaded, 16 * (b + 1))
                nc.scalar.activation(rows[:, par, :], rows[:, par, :], ACT.Identity, bias=bo_g[:, :])\
                    .then_inc(residual_set, 1)

            def take_k(b, n):
                act.wait_ge(k_proj, 2 * b + n + 1)
                if n == 0 and (not isinstance(b, int) or b > 0):
                    act.wait_ge(k_lo, b)
                nc.scalar.activation(nat[:, n * HALF:(n + 1) * HALF], proj[n][:, :], ACT.Identity,
                                     bias=bias[:, 1:2]).then_inc(k_nat, 1)

            def high_k(b):
                act.wait_ge(k_nat, 2 * b + 2)
                if not isinstance(b, int) or b > 0:
                    act.wait_ge(k_moved, 64 * b)
                nc.scalar.activation(k_hl[:, 0, :], nat[:, :], ACT.Copy).then_inc(k_hi, 1)

            def take_q(b):
                for n in range(2):
                    act.wait_ge(q_proj, 2 * b + n + 1)
                    nc.scalar.activation(xn[:, n * HALF:(n + 1) * HALF], proj[n][:, :], ACT.Identity,
                                         bias=bias[:, 0:1]).then_inc(q_nat, 1)
                act.wait_ge(q_nat, 2 * b + 2)
                if not isinstance(b, int) or b > 0:
                    act.wait_ge(q_moved, 64 * b)
                nc.scalar.activation(q_hl[:, 0, :], xn[:, :], ACT.Copy).then_inc(q_hi, 1)

            def high_v(b):
                act.wait_ge(v_nat, 3 * b + 3)
                if not isinstance(b, int) or b > 0:
                    act.wait_ge(v_placed, 224 * b)
                nc.scalar.activation(vn_hl[:, :, 0, :], vn[:, :, :], ACT.Copy).then_inc(v_hi, 1)

            def exp(b, g):
                act.wait_ge(shifted, G * b + g + 1)
                nc.scalar.activation(pr[:, g % 2], pr[:, g % 2], ACT.Exp, scale=HD ** -0.5)\
                    .then_inc(probs_ready, 1)
                act.wait_ge(probs_ready, G * b + g + 1)
                if not isinstance(b, int) or b > 0 or g >= NP:
                    act.wait_ge(probs_turned, G * b + g + 1 - NP)
                nc.scalar.activation(p_hl[:, g % NP, :, 0, 0:KW], pr[:, g % 2], ACT.Copy).then_inc(p_hi, 1)

            def take_pT(b, g):
                act.wait_ge(probs_turned, G * b + g + 1)
                if not isinstance(b, int) or b > 0 or g >= 2:
                    act.wait_ge(pv_ready, G * b + g - 1)
                nc.scalar.activation(pT[:, g % 2, :], turned[g % 2], ACT.Copy).then_inc(pT_ready, 1)

            def pick(b, g):
                q, hg = g // 2, g % 2
                act.wait_ge(pv_ready, G * b + g + 1)
                if g == 0 and (not isinstance(b, int) or b > 0):
                    act.wait_ge(oT_ready, b)
                src = mixed[g % 2].rearrange("p (j c) -> p j c", c=GC)
                for h in range(HG):
                    lo = QB * h
                    last = nc.scalar.activation(on[lo:lo + QB, hg, q * JQ:(q + 1) * JQ, :],
                                                src[lo:lo + QB, :, HD * h:HD * h + HD], ACT.Copy)
                last.then_inc(picked, 1)

            def take_xT(b):
                for n in range(2):
                    act.wait_ge(xT_ready, 2 * b + n + 1)
                    nc.scalar.activation(xT[:, bass.ds(b, 1), 0, 4 * n:4 * n + 4, :].rearrange("p a k r -> p (a k r)"),
                                         proj[n][:, :], ACT.Copy, scale=XS).then_inc(hi_ready, 1)

            def cast_piece(c, n, par):
                act.wait_ge(zero_taken, c * NPC + n + 1)
                if n < NGU:
                    if not isinstance(c, int) or c >= 2:
                        act.wait_ge(unit_ready, (c - 1) * NQT * QG)
                    k = n // 2 % 2 * KH
                    dst = w_int[:, par, n // 4, n % 2, k:k + KH, :].rearrange("p k i -> p (k i)")
                else:
                    if not isinstance(c, int) or c >= 2:
                        act.wait_ge(down_ready, (c - 1) * NQT * NCT + 1)
                    col = n % 2 * HALF
                    dst = d_int[:, par, (n - NGU) // 2, col:col + HALF]
                nc.scalar.activation(dst, raw_z[:, n % 2].rearrange("p k i -> p (k i)"), ACT.Copy).then_inc(w_cast, 1)

            take_k(0, 0)
            take_k(0, 1)
            high_k(0)
            take_q(0)
            high_v(0)
            act.wait_ge(s_turned, 1)
            nc.scalar.activation(scales[:, :, 0:2, :].rearrange("p n m k -> p n (m k)"),
                                 bank[7][:, 0:F // P * 2 * NK].rearrange("p (n mk) -> p n mk", mk=2 * NK),
                                 ACT.Copy).then_inc(s_kept, 1)
            nc.scalar.activation(scales[:, :, 2, :].rearrange("p n t -> p t n"),
                                 bank[6][:, 0:NCT * (F // P)].rearrange("p (t n) -> p t n", t=NCT),
                                 ACT.Copy).then_inc(s_kept, 1)

            def batch(b, par, prev, next):
                for g in range(G):
                    for at in lag(b, g, 4, prev):
                        pick(*at)
                    if g == 0 and prev >= 2:
                        take_xT(b - 2)
                    if g == 1 and next:
                        take_k(b + 1, 0)
                    if g == 2 and next:
                        take_k(b + 1, 1)
                        high_k(b + 1)
                    if g == 3 and next:
                        take_q(b + 1)
                    exp(b, g)
                    for at in lag(b, g, 2, prev):
                        take_pT(*at)
                    if g == 4:
                        set_residual(b, par)
                    if g == 5 and next:
                        high_v(b + 1)
                    if not next and g in CAST_AT:
                        cast_piece(0, CAST_AT.index(g), 0)

            batches(act, batch)
            take_xT(B - 2)
            for g in range(4):
                for at in lag(B, g, 2, True) if g < 2 else ():
                    take_pT(*at)
                pick(B - 1, G - 4 + g)

            def take_scales(c, par):
                if not isinstance(c, int) or c >= 2:
                    act.wait_ge(summed, (c - 1) * NQT * QS)
                    act.wait_ge(d_summed, count(c - 1, -1, True))
                nc.scalar.activation(scale[:, par], scales[:, bass.ds(c * SC, SC)], ACT.Copy).then_inc(scale_ready, 1)

            def start(c, u, par):
                q, t, i, k, m = quarter(u)
                act.wait_ge(unit_ready, (c * NQT + q) * QG + m + 1)
                if u == 0:
                    act.wait_ge(scale_ready, c + 1)
                if m == 0 and (not isinstance(c, int) or c > 0 or q >= 2):
                    act.wait_ge(h_lo_ready, c * NQT + q - 1)
                nc.scalar.activation(acc[:, q % 2, m, :], pair[u % 4][:, :, :].rearrange("p h r -> p (h r)"),
                                     ACT.Copy, scale=scale[:, par, i, m, 0:1]).then_inc(acc_started, 1)

            def silu(c, q):
                act.wait_ge(summed, (c * NQT + q + 1) * QS - 1)
                nc.scalar.activation(acc[:, q % 2, 0, :], acc[:, q % 2, 0, :], ACT.Silu, scale=1.0 / XS)\
                    .then_inc(silu_ready, 1)

            def high_hidden(c, q):
                c, q = (c - 1, NQT - 1) if q < 0 else (c, q)
                act.wait_ge(hid_ready, c * NQT + q + 1)
                if not isinstance(c, int) or c > 0 or q >= 2:
                    act.wait_ge(down_ready, (c * NQT + q - 1) * NCT)
                nc.scalar.activation(h_hi[:, q % 2, :], acc[:, q % 2, 0, :], ACT.Copy).then_inc(h_hi_ready, 1)

            def scale_down(c, x, par, slot):
                n = count(c, x, False)
                act.wait_ge(down_ready, c * NQT * NCT + x + 1)
                if not isinstance(n, int) or n > 2:
                    act.wait_ge(d_added, n - 2)
                nc.scalar.activation(d_part[:, (count(0, x, False) - 1) % 2, :],
                                     pair[slot][:, :, :].rearrange("p h r -> p (h r)"), ACT.Copy,
                                     scale=scale[:, par, x // NCT % SC, 2, x % NCT:x % NCT + 1])\
                    .then_inc(d_scaled, 1)

            act.wait_ge(s_kept, 2)
            for n in range(len(CAST_AT), NGU - 2):
                cast_piece(0, n, 0)
            take_scales(0, 0)

            def one(c, par, first, last):
                for u in range(NU):
                    if u % QU < 2:
                        start(c, u, par)
                    if first and u == 1:
                        cast_piece(0, NGU - 2, 0)
                        cast_piece(0, NGU - 1, 0)
                    if first and u == LAST_XT:
                        take_xT(B - 1)
                    if u % QU == 3 and not (first and u == 3):
                        high_hidden(c, u // QU - 1)
                    if u % QU == QU - 2:
                        silu(c, u // QU)
                    x = down_unit(c, u)
                    if u % 3 == 2 and x is not None and not by_dve(x):
                        scale_down(c, x, par if x >= 0 else 1 - par, u % 4)
                    for cc, n in due(c, u, 5, last):
                        cast_piece(cc, n, 1 - par if n < NGU else par)
                    if u == NU - 3 and not last:
                        take_scales(c + 1, 1 - par)

            passes(act, one)
            high_hidden(NC, -1)
            for n, (kind, x) in enumerate(end):
                if kind == "down" and not by_dve(x):
                    scale_down(NC - 1, x, 1, n % 4)

        @block.vector
        def _(dve):

            def moments(b, src, which, s_stats, s_mv):
                for n in range(2):
                    nc.vector.bn_stats(out=stats[:, which, n, :], in_=src(n)).then_inc(s_stats, 1)
                both, = first_wait(dve, 2 * b + 2)
                dve.wait_ge(s_stats, both)
                nc.vector.bn_aggr(out=mv[:, which, :], in_=stats[:, which, :, :]).then_inc(s_mv, 1)

            def moments_x(b):
                loaded, before = first_wait(dve, 16 * (b + 1), b)
                dve.wait_ge(x_loaded, loaded)
                if not isinstance(b, int) or b > 0:
                    dve.wait_ge(x_normed, before)
                    dve.wait_ge(rstd_done, before)
                moments(b, lambda n: xt[:, n * HALF:(n + 1) * HALF], 0, stats_done, mv_done)

            def norm_x(b):
                dve.wait_ge(rstd_done, b + 1)
                if isinstance(b, int) and 0 < b <= 2:
                    dve.wait_ge(q_lo, b)
                if not isinstance(b, int) or b > 2:
                    dve.wait_ge(xT_ready, 2 * b - 4)
                nc.vector.tensor_scalar(xn[:, :], xt[:, :], mv[:, 0, 0:1], rstd[:, 0:1],
                                        ALU.subtract, ALU.mult).then_inc(x_normed, 1)

            def moments_row(b, par):
                whole, before = first_wait(dve, 2 * b + 2, b)
                dve.wait_ge(attended, whole)
                if not isinstance(b, int) or b > 0:
                    dve.wait_ge(row_normed, before)
                    dve.wait_ge(rstd2_done, before)
                moments(b, lambda n: rows[:, par, n * HALF:(n + 1) * HALF], 1, stats2_done, mv2_done)

            def norm_row(b, par, last):
                row = rows[:, par, :]
                dve.wait_ge(rstd2_done, b + 1)
                dve.wait_ge(q_lo, B if last else b + 3)
                if not isinstance(b, int) or b > 0:
                    dve.wait_ge(xT_ready, 2 * b)
                nc.vector.tensor_scalar(xn[:, :], row, mv[:, 1, 0:1], rstd[:, 1:2],
                                        ALU.subtract, ALU.mult).then_inc(row_normed, 1)

            def soften(b, g, v_end=False):
                s = score[g % 2][:, 0:JQ * KW].rearrange("p (j k) -> p j k", k=KW)
                dve.wait_ge(scores_ready, G * b + g + 1)
                nc.vector.tensor_reduce(rmax[:, g % 2, :], s, AX.X, ALU.max).then_inc(max_ready, 1)
                if v_end:
                    take_v(b + 1, 0)
                dve.wait_ge(max_ready, G * b + g + 1)
                if not isinstance(b, int) or b > 0 or g >= 2:
                    dve.wait_ge(sum_ready, G * b + g - 1)
                nc.vector.tensor_tensor(pr[:, g % 2], s, rmax[:, g % 2, :].unsqueeze(2).to_broadcast([P, JQ, KW]),
                                        ALU.subtract).then_inc(shifted, 1)

            def total(b, g):
                dve.wait_ge(folded, 2 * (G * b + g + 1))
                if g == 0 and (not isinstance(b, int) or b > 0):
                    dve.wait_ge(rinv_ready, b)
                nc.vector.tensor_reduce(rsum[:, g % 2, g // 2 * JQ:(g // 2 + 1) * JQ], pr[:, g % 2, :, 0:KW // 4],
                                        AX.X, ALU.add).then_inc(sum_ready, 1)

            def invert(b):
                dve.wait_ge(sum_ready, G * b + G)
                if not isinstance(b, int) or b > 0:
                    dve.wait_ge(o_scaled, b)
                nc.vector.reciprocal(rinv[:, :], rsum[:, :, :].rearrange("p g j -> p (g j)")).then_inc(rinv_ready, 1)

            def turn_o(b):
                dve.wait_ge(picked, G * (b + 1))
                dve.wait_ge(rinv_ready, b + 1)
                o = on[:, :, :, :].rearrange("p g j d -> p (g j) d")
                nc.vector.tensor_tensor(o, o, rinv[:, :].unsqueeze(2).to_broadcast([P, 2 * NJ, HD]), ALU.mult)\
                    .then_inc(o_scaled, 1)
                dve.wait_ge(o_scaled, b + 1)
                if not isinstance(b, int) or b > 0:
                    dve.wait_ge(o_proj, 2 * b)
                nc.vector.transpose(oT[:, :, :].rearrange("p g n -> p (g n)"),
                                    on[:, :, :, :].rearrange("p g j d -> p (g j d)")).then_inc(oT_ready, 1)

            def add_attention(b, par):
                dve.wait_ge(residual_set, b + 1)
                for jj in range(2):
                    dve.wait_ge(o_proj, 2 * b + jj + 1)
                    row = rows[:, par, :].rearrange("p (j e t) -> p j e t", e=2, t=QB)[:, :, jj, :]
                    nc.vector.scalar_tensor_tensor(
                        out=row, in0=proj[jj].rearrange("p (j t) -> p j t", t=QB), scalar=tanh_g[:, 0:1],
                        in1=row, op0=ALU.mult, op1=ALU.add).then_inc(attended, 1)

            def take_xT(b):
                for n in range(2):
                    dve.wait_ge(hi_ready, 2 * b + n + 1)
                    hi, lo = (xT[:, bass.ds(b, 1), m, 4 * n:4 * n + 4, :].rearrange("p a k r -> p (a k r)")
                              for m in range(2))
                    nc.vector.scalar_tensor_tensor(out=lo, in0=proj[n][:, :], scalar=XS, in1=hi,
                                                   op0=ALU.mult, op1=ALU.subtract).then_inc(lo_ready, 1)

            def take_v(b, n):
                dve.wait_ge(v_proj, 3 * b + n + 1)
                if n == 0 and (not isinstance(b, int) or b > 0):
                    dve.wait_ge(v_lo, b)
                if n == 0:
                    nc.vector.tensor_tensor(vn[0:WIN, 8, :], score[0][0:WIN, JQ * KW:HALF], bv_all[0:WIN, :],
                                            ALU.add).then_inc(v_nat, 1)
                else:
                    nc.vector.tensor_tensor(vn[:, 4 * n - 4:4 * n, :],
                                            proj[n - 1].rearrange("p (n c) -> p n c", c=C),
                                            bv_all[:, :].unsqueeze(1).to_broadcast([P, 4, C]), ALU.add)\
                        .then_inc(v_nat, 1)

            def spread_q(b, half):
                dve.wait_ge(q_moved, 64 * (b + 1))
                if not isinstance(b, int) or b > 0:
                    dve.wait_ge(scores_ready, G * (b - 1) + (half + 1) * (G // 2))
                n = NJ // 2
                for hg in range(2):
                    for h in range(HG):
                        last = nc.vector.tensor_scalar(
                            qm[:, hg, half * n:(half + 1) * n, h, :],
                            qs[:, hg, half * HALF:(half + 1) * HALF].rearrange("p (j t) -> p j t", t=QB),
                            head_of[:, h:h + 1], None, ALU.mult)
                last.then_inc(q_spread, 1)

            nc.vector.memset(vn[:, 8, :], 0.0).then_inc(vn_zeroed, 1)
            moments_x(0)
            norm_x(0)
            nc.vector.memset(vt[:, 0].rearrange("p j h c -> p (j h c)").bitcast(fp32), 0.0).then_inc(vt_zeroed, 1)
            dve.wait_ge(gates_ready, 1)
            dve.wait_ge(consts_loaded, 16 * N_CONST)
            dve.wait_ge(vn_zeroed, 1)
            for n in range(3):
                take_v(0, n)
            dve.wait_ge(masks_made, 9)
            spread_q(0, 0)

            def batch(b, par, prev, next):
                for g in range(G):
                    if g == 7 and next:
                        spread_q(b + 1, 0)
                    for at in lag(b, g, 2, prev):
                        total(*at)
                    soften(b, g, g == 2 and next)
                    if g == 1 and prev:
                        invert(b - 1)
                    if g == 0 and next:
                        moments_x(b + 1)
                    if g == 0 and prev >= 2:
                        take_xT(b - 2)
                    if g == 1 and next:
                        norm_x(b + 1)
                    if g == 2:
                        spread_q(b, 1)
                    if g == 3 and prev:
                        turn_o(b - 1)
                    if g == 4 and next:
                        take_v(b + 1, 1)
                        take_v(b + 1, 2)
                    if g == 5 and prev:
                        add_attention(b - 1, 1 - par)
                        moments_row(b - 1, 1 - par)
                    if g == 6 and prev:
                        norm_row(b - 1, 1 - par, not next)

            batches(dve, batch)
            take_xT(B - 2)
            total(B - 1, G - 2)
            total(B - 1, G - 1)
            invert(B - 1)
            turn_o(B - 1)

            def add_unit(c, u, par):
                q, t, i, k, m = quarter(u)
                n = (c * NQT + q) * QS + 2 * k + m - 2
                dve.wait_ge(unit_ready, (c * NQT + q) * QG + 2 * k + m + 1)
                if k == 1:
                    dve.wait_ge(acc_started, (c * NQT + q) * 2 + m + 1)
                else:
                    dve.wait_ge(summed, n - 1)
                into = acc[:, q % 2, m, :]
                nc.vector.scalar_tensor_tensor(
                    out=into, in0=pair[u % 4][:, :, :].rearrange("p h r -> p (h r)"),
                    scalar=scale[:, par, i, m, k:k + 1], in1=into, op0=ALU.mult, op1=ALU.add).then_inc(summed, 1)

            def hidden(c, q):
                dve.wait_ge(silu_ready, c * NQT + q + 1)
                dve.wait_ge(summed, (c * NQT + q + 1) * QS)
                nc.vector.scalar_tensor_tensor(out=acc[:, q % 2, 0, :], in0=acc[:, q % 2, 1, :], scalar=1.0 / XS,
                                               in1=acc[:, q % 2, 0, :], op0=ALU.mult, op1=ALU.mult)\
                    .then_inc(hid_ready, 1)

            def add_down(c, x, par, slot):
                n = count(c, x, True)
                dve.wait_ge(down_ready, c * NQT * NCT + x + 1)
                if not isinstance(n, int) or n > 1:
                    dve.wait_ge(d_summed, n - 1)
                else:
                    dve.wait_ge(oacc_zeroed, NCT)
                into = oacc[:, x % NCT, x // NCT // SC % NT, :]
                src = pair[slot][:, :, :].rearrange("p h r -> p (h r)")
                by = scale[:, par, x // NCT % SC, 2, x % NCT:x % NCT + 1]
                nc.vector.scalar_tensor_tensor(out=into, in0=src, scalar=by, in1=into,
                                               op0=ALU.mult, op1=ALU.add).then_inc(d_summed, 1)

            def finish(b, slot):
                dve.wait_ge(out_turned, b + 1)
                if b % TT == 0:
                    dve.wait_ge(row_back[b // TT], 16 * TT)
                nc.vector.scalar_tensor_tensor(
                    out=as_rows(b), in0=pair[slot][:, :, :].rearrange("p h r -> p (h r)"), scalar=tanh_g[:, 1:2],
                    in1=as_rows(b), op0=ALU.mult, op1=ALU.add).then_inc(out_ready, 1)

            def one(c, par, first, last):
                for u in range(NU):
                    if u % 3 < 2 and u % QU >= 3:
                        add_unit(c, u, par)
                    if first and u == LAST_ADD:
                        add_attention(B - 1, 1)
                        moments_row(B - 1, 1)
                    if first and u == LAST_NORM:
                        norm_row(B - 1, 1, True)
                    if first and u == LAST_XT:
                        take_xT(B - 1)
                    x = down_unit(c, u)
                    if u % 3 == 2 and x is not None and by_dve(x):
                        add_down(c, x, par if x >= 0 else 1 - par, u % 4)
                    if u % QU == QU - 1:
                        hidden(c, u // QU)

            passes(dve, one)
            for n, (kind, x) in enumerate(end):
                if kind == "out":
                    finish(x, n % 4)
                elif by_dve(x):
                    add_down(NC - 1, x, 1, n % 4)

        @block.tensor
        def _(pe):
            pe.wait_ge(masks_made, 9)
            pe.wait_ge(consts_loaded, 16 * N_CONST)

            def bank_free(free):
                for s, count in free:
                    if not isinstance(count, int) or count > 0:
                        pe.wait_ge(s, count)

            def project_q(b, free):
                pe.wait_ge(x_normed, b + 1)
                for n in range(2):
                    bank_free(free(n))
                    nc.tensor.matmul(proj[n][:, :], wq[:, :], xn[:, n * HALF:(n + 1) * HALF],
                                     start=True, stop=True).then_inc(q_proj, 1)

            def project_k(b, free, halves=(0, 1)):
                pe.wait_ge(ctx_loaded, 16 * (b + 1))
                for n in halves:
                    bank_free(free(n))
                    nc.tensor.matmul(proj[n][:, :], wk[:, :], ct[:, PAD + n * HALF:PAD + (n + 1) * HALF],
                                     start=True, stop=True).then_inc(k_proj, 1)

            def project_v(b, half, free):
                pe.wait_ge(ctx_loaded, 16 * (b + 1))
                bank_free(free)
                for j in range(4):
                    start = (4 * half + j) * P
                    last = nc.tensor.matmul(proj[half][:, j * C:(j + 1) * C], ct[:, start:start + P], wv[:, :],
                                            start=True, stop=True)
                last.then_inc(v_proj, 1)

            def project_v_end(b):
                pe.wait_ge(ctx_loaded, 16 * (b + 1))
                nc.tensor.matmul(score[0][0:QB, JQ * KW:HALF], ct[:, T:T + QB], wv[:, :], start=True, stop=True,
                                 skip_group_check=True).then_inc(v_proj, 1)

            def scores(b, g, par, v_end=False):
                q, hg = g // 2, g % 2
                if g == 0:
                    pe.wait_ge(k_moved, 64 * (b + 1))
                    pe.wait_ge(q_spread, 2 * b + 1)
                if g == G // 2:
                    pe.wait_ge(q_spread, 2 * b + 2)
                if not isinstance(b, int) or b > 0 or g >= 2:
                    pe.wait_ge(shifted, G * b + g - 1)
                if v_end:
                    project_v_end(b + 1)
                dst = score[g % 2][:, 0:JQ * KW].rearrange("p (j k) -> p j k", k=KW)
                nc.tensor.matmul(dst, spread[:, :, :].rearrange("p h t -> p (h t)"),
                                 window[:, :].unsqueeze(1).to_broadcast([P, JQ, KW]),
                                 start=True, stop=False, skip_group_check=True)
                for j in range(JQ):
                    t = QB * (JQ * q + j)
                    for part in range(2):
                        last = nc.tensor.matmul(dst[:, j, :], qm[:, hg, JQ * q + j, :, :].rearrange("p h t -> p (h t)"),
                                                ks[:, par, hg, part, t:t + KW], start=False,
                                                stop=(j == JQ - 1 and part == 1), skip_group_check=True)
                last.then_inc(scores_ready, 1)

            def turn_probs(b, g):
                pe.wait_ge(p_lo, G * b + g + 1)
                if not isinstance(b, int) or b > 0 or g >= 2:
                    pe.wait_ge(pT_ready, G * b + g - 1)
                for j in range(JQ):
                    last = nc.tensor.transpose(turned[g % 2][:, j * P:(j + 1) * P],
                                               p_hl[:, g % NP, j, :, :].rearrange("p h k -> p (h k)"), ident16[:, :])
                last.then_inc(probs_turned, 1)

            def mix(b, g, par):
                q, hg = g // 2, g % 2
                pe.wait_ge(pT_ready, G * b + g + 1)
                if g == 0:
                    pe.wait_ge(v_placed, 224 * (b + 1))
                if not isinstance(b, int) or b > 0 or g >= 2:
                    pe.wait_ge(picked, G * b + g - 1)
                k = KP + KW
                for j in range(JQ):
                    for part in range(2):
                        last = nc.tensor.matmul(mixed[g % 2][:, j * GC:(j + 1) * GC],
                                                pT[0:k, g % 2, j * P:(j + 1) * P],
                                                vt[0:k, par, q * JQ + j, part, hg * GC:(hg + 1) * GC],
                                                start=(part == 0), stop=(part == 1))
                last.then_inc(pv_ready, 1)

            def project_o(b, free):
                pe.wait_ge(oT_ready, b + 1)
                if isinstance(b, int) and b == 0:
                    pe.wait_ge(wo_loaded, 16 * 16)
                for jj in range(2):
                    bank_free(free(jj))
                    for hg in range(2):
                        last = nc.tensor.matmul(proj[jj][:, :], wo[:, hg, jj, :], oT[:, hg, :],
                                                start=(hg == 0), stop=(hg == 1))
                    last.then_inc(o_proj, 1)

            def turn_x(b, free):
                pe.wait_ge(row_normed, b + 1)
                for n in range(2):
                    bank_free(free(n))
                    for k in range(4):
                        f = (4 * n + k) * P
                        last = nc.tensor.transpose(proj[n][:, k * P:(k + 1) * P], xn[:, f:f + P], ident[:, :])
                    last.then_inc(xT_ready, 1)

            project_k(0, lambda n: [])
            project_q(0, lambda n: [(k_nat, n + 1)])
            project_v_end(0)
            project_v(0, 0, [(q_nat, 1)])
            project_v(0, 1, [(q_nat, 2)])
            pe.wait_ge(s_loaded, 48)
            for n in range(F // P):
                last = nc.tensor.transpose(bank[7][:, n * 2 * NK:(n + 1) * 2 * NK], gu_stage[0:2 * NK, n * P:(n + 1) * P],
                                           ident[0:2 * NK, 0:2 * NK])
            for n in range(NCT):
                last = nc.tensor.transpose(bank[6][:, n * (F // P):(n + 1) * (F // P)],
                                           d_stage[0:F // P, n * P:(n + 1) * P], ident[0:F // P, 0:F // P])
            last.then_inc(s_turned, 1)
            pe.wait_ge(v_nat, 3)
            pe.wait_ge(s_kept, 2)

            def batch(b, par, prev, next):
                for g in range(G):
                    scores(b, g, par, g == 2 and next)
                    if g == 0 and prev >= 2:
                        turn_x(b - 2, lambda n: [(attended, 2 * b + n - 3)])
                    if g in (1, 2) and next:
                        project_k(b + 1, lambda n: [(lo_ready, 2 * b + n - 3) if prev >= 2 else (v_nat, 3 * b + 3)],
                                  (g - 1,))
                    if g == 3 and next:
                        project_q(b + 1, lambda n: [(k_nat, 2 * b + n + 3)])
                    if g == 4 and next:
                        project_v(b + 1, 0, [(q_nat, 2 * b + 3)])
                        project_v(b + 1, 1, [(q_nat, 2 * b + 4)])
                    if g == 5 and prev:
                        project_o(b - 1, (lambda n: [(v_nat, 3 * b + 5 + n)]) if next else
                                  (lambda n: [(lo_ready, 2 * b + n - 3)]))
                    for at in lag(b, g, 2, prev):
                        turn_probs(*at)
                    for at in lag(b, g, 3, prev):
                        mix(*at, par if g >= 3 else 1 - par)

            batches(pe, batch)
            turn_x(B - 2, lambda n: [(attended, 2 * B + n - 3)])
            for g in range(3):
                for at in lag(B, g, 2, True) if g < 2 else ():
                    turn_probs(*at)
                mix(B - 1, G - 3 + g, 1)

            pe.wait_ge(lo_ready, 2 * B - 2)
            pe.wait_ge(shifted, G * B)
            pe.wait_ge(pT_ready, G * B)
            pe.wait_ge(picked, G * B)

            def integer_product(dst, weights, rows_of):
                for h in range(2):
                    for part in range(2):
                        last = nc.tensor.matmul(dst[:, h, :], weights, rows_of(h, part),
                                                start=(part == 0), stop=(part == 1))
                return last

            def gate_up(c, u, par):
                q, t, i, k, m = quarter(u)
                if t == 0 and k in (0, KH):
                    pe.wait_ge(w_cast, c * NPC + 4 * i + (1 + m if k == 0 else 3 + m))
                half = TT // 2
                integer_product(pair[u % 4], w_int[:, par, i, m, k, :],
                                lambda h, part: xT[:, t * TT + h * half:t * TT + (h + 1) * half, part, k, :])\
                    .then_inc(unit_ready, 1)

            def down(c, x, par, slot):
                q, i = x // NCT, x // NCT % SC
                if x % NCT == 0:
                    pe.wait_ge(h_lo_ready, c * NQT + q + 1)
                    if q // SC % NT == 0:
                        pe.wait_ge(w_cast, c * NPC + NGU + 2 * i + 2)
                col = x % NCT * P
                integer_product(pair[slot], d_int[:, par, i, col:col + P],
                                lambda h, part: (h_hi, h_lo)[part][:, q % 2, h * HALF:(h + 1) * HALF])\
                    .then_inc(down_ready, 1)

            def turn_out(b, slot):
                if b % TT == 0:
                    x = NQT * NCT - 1 - (NT - 1 - b // TT) * SC * NCT
                    pe.wait_ge(d_summed, count(NC - 1, x, True))
                    pe.wait_ge(d_added, count(NC - 1, x, False))
                r = b % TT * P
                for ct_ in range(NCT):
                    last = nc.tensor.transpose(pair[slot][:, ct_ // 4, ct_ % 4 * P:(ct_ % 4 + 1) * P],
                                               oacc[:, ct_, b // TT, r:r + P], ident[:, :])
                last.then_inc(out_turned, 1)

            def one(c, par, first, last):
                for u in range(NU):
                    x = down_unit(c, u)
                    if first and u in (LAST_O, LAST_TURN):
                        pe.wait_ge(*emptied(c, u))
                        project_o(B - 1, lambda n: []) if u == LAST_O else turn_x(B - 1, lambda n: [])
                    if u % 3 == 2 and x is None:
                        continue
                    if first and u == LAST_O + 4:
                        pe.wait_ge(attended, 2 * B)
                    if first and u == LAST_TURN + 4:
                        pe.wait_ge(lo_ready, 2 * B)
                    wait = emptied(c, u)
                    if wait:
                        pe.wait_ge(*wait)
                    if u % 3 < 2:
                        gate_up(c, u, par)
                    else:
                        down(c, x, par if x >= 0 else 1 - par, u % 4)

            passes(pe, one)
            for n, (kind, x) in enumerate(end):
                pe.wait_ge(*end_emptied(n))
                if kind == "down":
                    down(NC - 1, x, 1, n % 4)
                else:
                    turn_out(x, n % 4)


_INS = ['x', 'ctx_4096', 'g_xattn', 'g_ffn', 'L0_xattn_Wq', 'L0_xattn_bq', 'L0_xattn_Wk', 'L0_xattn_bk',
        'L0_xattn_Wv', 'L0_xattn_bv', 'L0_xattn_Wo', 'L0_xattn_bo', 'L0_ffn_gate_w', 'L0_ffn_gate_z',
        'L0_ffn_gate_s', 'L0_ffn_up_w', 'L0_ffn_up_z', 'L0_ffn_up_s', 'L0_ffn_down_w', 'L0_ffn_down_z',
        'L0_ffn_down_s']
_TRANSPOSED = ('L0_xattn_Wq', 'L0_xattn_Wk', 'L0_xattn_Wv', 'L0_xattn_Wo')


def kernel(**inputs):
    import numpy as _np
    import concourse.bacc as _bacc
    from concourse import mybir as _mybir
    from concourse.bass_utils import run_bass_kernel_spmd as _run

    nc = _bacc.Bacc("TRN2", target_bir_lowering=False, num_devices=1)
    arrays, args = {}, []
    for name in _INS:
        a = _np.asarray(inputs[name])
        a = _np.ascontiguousarray(a.T if name in _TRANSPOSED else a)
        arrays[f"in_{name}_dram"] = a
        args.append(nc.dram_tensor(f"in_{name}_dram", a.shape, _mybir.dt.from_np(a.dtype), kind="ExternalInput").ap())
    args.append(nc.dram_tensor("out_0_dram", (16, 128, 1024), _mybir.dt.float32, kind="ExternalOutput").ap())
    flamingo_layer(nc, *args)
    r = _run(nc, [arrays], core_ids=[0])
    return r.results[0]["out_0_dram"]
```
